# Optimizing a Trainium2 kernel written in Bass

```python
import numpy as np
import jax
import jax.numpy as jnp

def _softmax(x, axis=-1):
    return jax.nn.softmax(x, axis=axis)

def _gelu(x):
    return jax.nn.gelu(x, approximate=True)

def _silu(x):
    return jax.nn.silu(x)

def _sigmoid(x):
    return jax.nn.sigmoid(x)

def _layernorm(x, axis=-1, eps=1e-05):
    m = jnp.mean(x, axis=axis, keepdims=True)
    v = jnp.var(x, axis=axis, keepdims=True)
    return (x - m) / jnp.sqrt(v + eps)

def _scatter_add(tgt, idx, src, axis=0):
    return tgt.at[idx].add(src)

def _segment_sum(src, seg, n):
    return jax.ops.segment_sum(src, seg, n)
kernel_name = 'mk_gnn_resnorm_d2_gnn_r8_4248de'

def setup_inputs(seed: int=0):
    np.random.seed(seed)
    _w = jnp.asarray

    def _rec_inputs():
        import jax
        import jax.numpy as jnp
        _gk = jax.random.key(seed)
        x = -0.0001006 + 1 * jax.random.normal(jax.random.fold_in(_gk, 1), (12500, 48), jnp.float32)
        src = jax.random.randint(jax.random.fold_in(_gk, 2), (200000,), 0, 12500, jnp.int32)
        dst = jax.random.randint(jax.random.fold_in(_gk, 3), (200000,), 0, 12500, jnp.int32)
        _o = jnp.argsort(dst, stable=True)
        src = src[_o]
        dst = dst[_o]
        edge_attr_32 = 0.000189758 + 1.00013 * jax.random.normal(jax.random.fold_in(_gk, 12), (200000, 32), jnp.float32)
        edge_attr_48 = -4.21973e-05 + 0.999841 * jax.random.normal(jax.random.fold_in(_gk, 13), (200000, 48), jnp.float32)
        return (x, src, dst, edge_attr_32, edge_attr_48)
    x, src, dst, edge_attr_32, edge_attr_48 = _rec_inputs()

    def _L0_gnn_setup():
        import jax, jax.numpy as jnp
        import numpy as np
        N_NODES = 12500
        key = jax.random.key(seed)
        k1, k2, k3, k4, k5, k6 = jax.random.split(key, 6)
        node_dim, edge_dim, hidden = (48, 32, 128)
        E = 200000
        x = jax.random.normal(k1, (N_NODES, node_dim), dtype=jnp.float32)
        edge_index = jax.random.randint(k2, (2, E), 0, N_NODES, dtype=jnp.int64)
        edge_attr = jax.random.normal(k3, (E, edge_dim), dtype=jnp.float32)
        in_dim = 2 * node_dim + edge_dim
        s1 = 1.0 / np.sqrt(in_dim)
        s2 = 1.0 / np.sqrt(hidden)
        W1 = jax.random.uniform(k4, (in_dim, hidden), minval=-s1, maxval=s1, dtype=jnp.float32)
        b1 = jax.random.uniform(k5, (hidden,), minval=-s1, maxval=s1, dtype=jnp.float32)
        W2 = jax.random.uniform(k6, (hidden, node_dim), minval=-s2, maxval=s2, dtype=jnp.float32)
        b2 = jnp.zeros((node_dim,), dtype=jnp.float32)
        return {'x': x, 'edge_index': edge_index, 'edge_attr': edge_attr, 'W1': W1, 'b1': b1, 'W2': W2, 'b2': b2}
    _L0_gnn_all = _L0_gnn_setup()
    _L0_gnn_in = {k: v for k, v in _L0_gnn_all.items() if k in ('W1', 'b1', 'W2', 'b2')}
    del _L0_gnn_all

    def _L1_gnn_setup():
        import jax, jax.numpy as jnp
        import numpy as np
        N_NODES = 12500
        N_EDGES = 200000
        D_FEAT = 48
        key = jax.random.key(seed)
        k1, k2, k3, k4 = jax.random.split(key, 4)
        node_feat = jax.random.normal(k1, (N_NODES, D_FEAT), dtype=jnp.float32)
        edge_feat = jax.random.normal(k2, (N_EDGES, D_FEAT), dtype=jnp.float32)
        src = jax.random.randint(k3, (N_EDGES,), 0, N_NODES, dtype=jnp.int32)
        dst = jax.random.randint(k4, (N_EDGES,), 0, N_NODES, dtype=jnp.int32)
        eps = jnp.zeros((1,), dtype=jnp.float32)
        return {'node_feat': node_feat, 'edge_feat': edge_feat, 'src': src, 'dst': dst, 'eps': eps}
    _L1_gnn_all = _L1_gnn_setup()
    _L1_gnn_in = {k: v for k, v in _L1_gnn_all.items() if k in ('eps',)}
    del _L1_gnn_all
    return {'x': x, 'src': src, 'dst': dst, 'edge_attr_32': edge_attr_32, 'edge_attr_48': edge_attr_48, 'L0_gnn_W1': _L0_gnn_in['W1'], 'L0_gnn_b1': _L0_gnn_in['b1'], 'L0_gnn_W2': _L0_gnn_in['W2'], 'L0_gnn_b2': _L0_gnn_in['b2'], 'L1_gnn_eps': _L1_gnn_in['eps']}

def reference(x, src, dst, edge_attr_32, edge_attr_48, L0_gnn_W1, L0_gnn_b1, L0_gnn_W2, L0_gnn_b2, L1_gnn_eps):
    import jax
    import jax.numpy as jnp

    def _L0_gnn_ref(x, edge_index, edge_attr, W1, b1, W2, b2):
        import jax, jax.numpy as jnp
        import numpy as np
        N_NODES = 12500
        src, dst = (edge_index[0], edge_index[1])
        x_i = x[dst]
        x_j = x[src]
        tmp = jnp.concatenate([x_i, x_j, edge_attr], axis=1)
        h = jax.nn.relu(tmp @ W1 + b1)
        msg = h @ W2 + b2
        out = jax.ops.segment_sum(msg, dst, num_segments=N_NODES)
        return out

    def _L1_gnn_ref(node_feat, edge_feat, src, dst, eps):
        import jax, jax.numpy as jnp
        import numpy as np
        N_NODES = 12500
        N_EDGES = 200000
        D_FEAT = 48
        m = jax.nn.relu(node_feat[src] + edge_feat)
        neigh = jax.ops.segment_sum(m, dst, num_segments=N_NODES)
        return (1.0 + eps[0]) * node_feat + neigh
    edge_index = jnp.stack([src, dst])
    x = _layernorm(x + _L0_gnn_ref(x, edge_index, edge_attr_32, L0_gnn_W1, L0_gnn_b1, L0_gnn_W2, L0_gnn_b2), axis=-1)
    x = _layernorm(x + _L1_gnn_ref(x, edge_attr_48, src, dst, L1_gnn_eps), axis=-1)
    return x

_drawn_inputs = setup_inputs


def setup_inputs(seed=0):
    import zlib

    import numpy as np

    out = dict(_drawn_inputs(seed))
    spreads = {'L0_gnn_b2': (0.0, 0.1)}
    factors = {}
    for name, (base, spread) in spreads.items():
        noise = np.random.default_rng([zlib.crc32(name.encode()), seed]).standard_normal(out[name].shape)
        drawn = base * np.exp(spread * noise) if base else spread * noise
        out[name] = jnp.asarray(drawn.astype(out[name].dtype))
    for name, factor in factors.items():
        out[name] = (out[name] * factor).astype(out[name].dtype)
    return out
```

```python
from contextlib import ExitStack

import concourse.bass as bass
from concourse import mybir

F32 = mybir.dt.float32
I32 = mybir.dt.int32
U32 = mybir.dt.uint32
ALU = mybir.AluOpType
ACT = mybir.ActivationFunctionType
AX = mybir.AxisListType

N = 12500
D = 48
DE = 32
H = 128
E = 200000
P = 128
TILES = 4
GE = P * TILES
UNROLL = 4
WIN = 48
GROUPS = -(-E // (GE * UNROLL)) * UNROLL
ITERS = GROUPS // UNROLL
EPAD = GROUPS * GE
HALVES = GROUPS // 2
GP = GROUPS // 4
BLK = 100
NP = N // BLK
CHUNKS = 10
CB = BLK // CHUNKS
NBANKS = 4
ACCW = P * ITERS
XROWS = N + 1
TROWS = -(-(XROWS + P) // P) * P
NORM_EPS = 1e-5
assert NP * BLK == N and ACCW >= N and GP <= P and CB * D <= GE and WIN + D + DE == P
assert 4 * GE + GROUPS * TILES + TROWS // P * D <= ACCW


def build(nc, x, xT, src_tiles, dst_tiles, dst_groups, e32, e48, w1, w2, b1, b2, eps, ident, iota, center,
          earlier, spare, out):
    ctx = ExitStack()
    with ctx:
        def sb(name, shape, dt=F32):
            return ctx.enter_context(nc.sbuf_tensor(name, shape, dt))

        def pb(name, shape, dt=F32):
            return ctx.enter_context(nc.psum_tensor(name, shape, dt))

        def sem(name):
            return ctx.enter_context(nc.semaphore(name))

        def sems(name, n):
            return [sem(f"{name}{k}") for k in range(n)]

        x1_dram = nc.dram_tensor("x1_dram", (N, D), F32, kind="Internal").ap()
        table = [nc.dram_tensor(f"table{n}_dram", (TROWS, D), F32, kind="Internal").ap() for n in range(2)]

        ident_sb = sb("ident_sb", [P, P])
        iota_sb = sb("iota_sb", [P, WIN])
        center_sb = sb("center_sb", [D, D])
        w1_dst = sb("w1_dst", [D, H])
        w2_sb = sb("w2_sb", [H, D])
        b1_sb = sb("b1_sb", [H, 1])
        b2_sb = sb("b2_sb", [P, D])
        res_scale = sb("res_scale", [P, 1])
        norm_eps = sb("norm_eps", [P, 1])
        zeros = sb("zeros", [D, P])
        ones = sb("ones", [GP, P])
        low = sb("low", [GP, 4])
        high = sb("high", [GP, 4])
        base = sb("base", [GP, 4])
        wide = sb("wide", [GP, 4])
        spread = sb("spread", [GP, GP, 4])
        base_row = sb("base_row", [1, GROUPS], I32)
        n_wide = sb("n_wide", [1, 1])
        n_wide_i = sb("n_wide_i", [1, 1], I32)
        rel = sb("rel", [P, GROUPS + 1, TILES])
        idx = sb("idx", [P, UNROLL, TILES], U32)
        edge = sb("edge", [P, UNROLL, TILES, P])
        e48_sb = sb("e48_sb", [P, UNROLL, TILES, D])
        x_win = sb("x_win", [D, UNROLL, WIN])
        w_edge = sb("w_edge", [P, UNROLL, H])
        edgeT = sb("edgeT", [P, 2, GE])
        hT = sb("hT", [H, 2, GE])
        pre1 = sb("pre1", [P, 2, TILES, D])
        msg = sb("msg", [P, 2, TILES, D])
        acc = [sb("acc0", [D, ACCW]), sb("acc1", [P, ACCW])]
        dst_g = acc[1][0:GP, 0:4 * GE].bitcast(I32)
        dst_t = acc[1][:, 4 * GE:4 * GE + GROUPS * TILES].bitcast(I32)
        zero_table = acc[1][:, 4 * GE + GROUPS * TILES:4 * GE + GROUPS * TILES + TROWS // P * D]
        feats = sb("feats", [NP, BLK, D])
        resid = sb("resid", [NP, BLK, D])
        square = sb("square", [NP, 2, CB, D])
        mean = sb("mean", [NP, BLK])
        var = sb("var", [NP, BLK])
        std = sb("std", [NP, BLK])
        rstd = sb("rstd", [NP, BLK])
        dst_idx = sb("dst_idx", [P, TILES], U32)
        dst_f = sb("dst_f", [P, TILES])
        w_full = sb("w_full", [P, H])
        earlier_sb = sb("earlier_sb", [P, P])
        spare_sb = sb("spare_sb", [P, 1])
        same = sb("same", [P, P])
        same_earlier = sb("same_earlier", [P, P])
        n_earlier = sb("n_earlier", [P, 1])
        to_spare = sb("to_spare", [P, 1])
        target = sb("target", [P, 1], U32)
        addend = sb("addend", [P, D])

        ps_t = [pb(f"ps_t{k}", [P, GE]) for k in range(2)]
        ps_h = [pb(f"ps_h{k}", [H, GE]) for k in range(2)]
        ps_a = pb("ps_a", [WIN, H])
        ps_m = pb("ps_m", [P, TILES, D])
        ps_s = pb("ps_s", [D, WIN])
        ps_nodes = [*ps_t, *ps_h]
        ps_row, ps_merged = ps_t[1][:, 0:P], ps_h[1][:, 0:D]

        s_dst_g = sem("s_dst_g")
        s_dst_t = sem("s_dst_t")
        s_ident = sem("s_ident")
        s_const = sem("s_const")
        s_set = sem("s_set")
        s_spread = sem("s_spread")
        s_wide = sem("s_wide")
        s_windows = sem("s_windows")
        s_n_wide = sem("s_n_wide")
        s_known = sem("s_known")
        s_prologue = sem("s_prologue")
        s_narrow = sem("s_narrow")
        s_general = sem("s_general")
        s_passed = sem("s_passed")
        s_xT = sem("s_xT")
        s_x = sem("s_x")
        s_x1 = sem("s_x1")
        s_out = sem("s_out")
        N_CONST = 14

        def layer_sems(n):
            per_slot = {"idx": 2, "edges": 2, "window": UNROLL, "rows": UNROLL}
            counts = ("onehot", "awin", "stat", "trans", "edgeT", "pre", "h", "msgp", "sum", "msg", "seg", "acc",
                      "nodes", "resid", "square", "var", "std", "norm")
            return {**{w: sems(f"s{n}_{w}", k) for w, k in per_slot.items()}, **{w: sem(f"s{n}_{w}") for w in counts}}

        def general_sems(n):
            counts = ("zeroed", "table", "idx", "edges", "dst", "rows", "trans", "edgeT", "pre", "h", "msgp", "sum",
                      "msg", "row", "same", "merged", "addend", "added", "step")
            return {w: sem(f"g{n}_{w}") for w in counts}

        S0, S1 = layer_sems(0), layer_sems(1)
        G0, G1 = general_sems(0), general_sems(1)
        block = ctx.enter_context(nc.Block())

        def wait_group(eng, s, i, u, back=0):
            if isinstance(i, int) and UNROLL * i + u - back < 0:
                return
            eng.wait_ge(s, i * UNROLL + (u - back + 1))

        def wait_count(eng, s, h, per, n):
            if isinstance(h, int) and per * h + n <= 0:
                return
            eng.wait_ge(s, h * per + n)

        def peeled(eng, body, count=ITERS):
            body(0)
            with eng.Fori(1, count) as i:
                body(i)

        def first_group(i, u):
            return isinstance(i, int) and i == 0 and u == 0

        def by_width(eng, general, windowed):
            eng.wait_ge(s_known, 2)
            wide_groups = eng.value_load(n_wide_i[0:1, 0:1], min_val=0, max_val=GROUPS)
            with eng.If(wide_groups > 0):
                general()
            with eng.Else():
                windowed()

        def store_nodes(sp, S, dram, done):
            nodes = dram.rearrange("(p k) f -> p k f", p=NP)
            for c in range(CHUNKS):
                sp.wait_ge(S["norm"], c + 1)
                sp.dma_start(nodes[:, c * CB:(c + 1) * CB, :], feats[:, c * CB:(c + 1) * CB, :]).then_inc(done, 16)

        @block.sync
        def _(sp):
            def load_idx(done, i, h, slot):
                sp.dma_start(idx[:, slot:slot + 2, :].rearrange("p g t -> p (g t)"),
                             src_tiles[:, bass.ds(i * (UNROLL * TILES) + h * 2 * TILES, 2 * TILES)]).then_inc(done, 16)

            def load_e32(done, half, slot):
                sp.dma_start(edge[:, slot:slot + 2, :, 2 * D:P].rearrange("p g t f -> p (g t) f"),
                             e32[bass.ds(half, 1), :, :].rearrange("a p (t f) -> (a p) t f", f=DE)).then_inc(done, 16)

            def load_e48(done, half, slot):
                sp.dma_start(e48_sb[:, slot:slot + 2, :, :].rearrange("p g t f -> p (g t f)"),
                             e48[bass.ds(half, 1), :, :].rearrange("a p n -> (a p) n")).then_inc(done, 16)

            load_idx(S0["idx"][0], 0, 0, 0)
            sp.dma_start(dst_g, dst_groups).then_inc(s_dst_g, 16)
            load_idx(S0["idx"][1], 0, 1, 2)
            sp.dma_start(dst_t, dst_tiles).then_inc(s_dst_t, 16)

            def loads0(i):
                for u in range(UNROLL):
                    if u % 2 == 0:
                        wait_group(sp, S0["trans"], i, u + 1, back=UNROLL)
                        if not isinstance(i, int):
                            load_idx(S0["idx"][u // 2], i, u // 2, u)
                        load_e32(S0["edges"][u // 2], i * 2 + u // 2, u)
                    wait_group(sp, S0["awin"], i, u, back=UNROLL)
                    first = sp.value_load(base_row[0:1, bass.ds(i * UNROLL + u, 1)], min_val=0, max_val=N - WIN)
                    sp.dma_start(x_win[:, u, :], xT[:, bass.ds(first, WIN)]).then_inc(S0["window"][u], 16)

            def loads1(i):
                for h in range(2):
                    wait_group(sp, S1["sum"], i, 2 * h + 1, back=UNROLL)
                    load_idx(S1["idx"][h], i, h, 2 * h)
                    load_e48(S1["edges"][h], i * 2 + h, 2 * h)

            def windowed():
                peeled(sp, loads0)
                sp.wait_ge(S0["trans"], GROUPS)
                loads1(0)
                store_nodes(sp, S0, x1_dram, s_x1)
                with sp.Fori(1, ITERS) as i:
                    loads1(i)
                store_nodes(sp, S1, out, s_out)
                sp.wait_ge(s_x1, 16 * CHUNKS)
                sp.wait_ge(s_out, 16 * CHUNKS)

            def general_layer(G, n):
                def loads(h):
                    wait_count(sp, G["added"], h, 32 * TILES, 0)
                    sp.dma_start(idx[:, 0:2, :].rearrange("p g t -> p (g t)"),
                                 src_tiles[:, bass.ds(h * 2 * TILES, 2 * TILES)]).then_inc(G["idx"], 16)
                    (load_e48 if n else load_e32)(G["edges"], h, 0)

                sp.wait_ge(G["zeroed"], 1)
                sp.dma_start(table[n].rearrange("(p r) f -> p (r f)", p=P), zero_table).then_inc(G["table"], 16)
                peeled(sp, loads, HALVES)
                sp.wait_ge(G["added"], 16 * TILES * GROUPS)
                sp.wait_ge(G["table"], 16)
                sp.dma_start(resid[:, :, :].rearrange("p k f -> p (k f)"),
                             table[n][0:N, :].rearrange("(p k) f -> p (k f)", p=NP)).then_inc(G["table"], 16)

            def general():
                for u in range(UNROLL):
                    sp.wait_ge(S0["rows"][u], 16 * TILES)
                sp.dma_start(feats[:, :, :].rearrange("p k f -> p (k f)"),
                             x[0:N, :].rearrange("(p k) f -> p (k f)", p=NP)).then_inc(s_x, 16)
                general_layer(G0, 0)
                store_nodes(sp, S0, x1_dram, s_x1)
                sp.wait_ge(s_x1, 16 * CHUNKS)
                general_layer(G1, 1)
                store_nodes(sp, S1, out, s_out)
                sp.wait_ge(s_out, 16 * CHUNKS)

            by_width(sp, general, windowed)

        @block.gpsimd
        def _(pool):
            def gather(cols, rows_of, index, done):
                pool.indirect_dma_start(out=cols, out_offset=None, in_=rows_of,
                                        in_offset=bass.IndirectOffsetOnAxis(ap=index, axis=0)).then_inc(done, 16)

            def gathers(S, rows_of, read, i):
                for u in range(UNROLL):
                    pool.wait_ge(S["idx"][u // 2], i * 16 + 16)
                    wait_group(pool, S[read], i, u, back=UNROLL)
                    pool.sem_inc(s_passed, 1)
                    for t in range(TILES):
                        gather(edge[:, u, t, D:2 * D], rows_of, idx[:, u, t:t + 1], S["rows"][u])

            gathers(S0, x, "trans", 0)

            def windowed():
                with pool.Fori(1, ITERS) as i:
                    gathers(S0, x, "trans", i)
                pool.wait_ge(s_x1, 16 * CHUNKS)
                peeled(pool, lambda i: gathers(S1, x1_dram, "sum", i))

            def general_layer(G, n):
                def steps(h):
                    for u in range(2):
                        pool.wait_ge(G["idx"], h * 16 + 16)
                        wait_count(pool, G["dst"], h, 2, u + 1)
                        pool.sem_inc(s_passed, 1)
                        for t in range(TILES):
                            gather(edge[:, u, t, D:2 * D], x1_dram if n else x, idx[:, u, t:t + 1], G["rows"])
                            if n == 0:
                                gather(edge[:, u, t, 0:D], x, dst_idx[:, t:t + 1], G["rows"])
                        for t in range(TILES):
                            wait_count(pool, G["addend"], h, 2 * TILES, u * TILES + t + 1)
                            pool.sem_inc(s_passed, 1)
                            pool.indirect_dma_start(out=table[n], in_=addend[:, :], in_offset=None, compute_op=ALU.add,
                                                    out_offset=bass.IndirectOffsetOnAxis(ap=target[:, :], axis=0),
                                                    ).then_inc(G["added"], 16)

                pool.wait_ge(G["table"], 16)
                peeled(pool, steps, HALVES)

            def general():
                for u in range(UNROLL):
                    pool.wait_ge(S0["rows"][u], 16 * TILES)
                general_layer(G0, 0)
                pool.wait_ge(s_x1, 16 * CHUNKS)
                general_layer(G1, 1)

            by_width(pool, general, windowed)

        @block.scalar
        def _(act):
            act.dma_start(ident_sb[:, :], ident).then_inc(s_ident, 16)
            for dst, src in ((iota_sb, iota), (w1_dst, w1[0:D, :]), (w2_sb, w2), (b1_sb, b1),
                             (b2_sb, b2.to_broadcast([P, D])), (res_scale, eps.to_broadcast([P, 1])),
                             (center_sb, center), (w_full, w1), (earlier_sb, earlier), (spare_sb, spare)):
                act.dma_start(dst[:, :], src).then_inc(s_const, 16)
            for u in range(UNROLL):
                act.dma_start(w_edge[D:P, u, :], w1[D:P, :]).then_inc(s_const, 16)
            act.dma_start(acc[0][:, 0:N], xT).then_inc(s_xT, 16)
            act.wait_ge(s_const, 16 * N_CONST)

            def steps0(i):
                for u in range(UNROLL):
                    wait_group(act, S0["pre"], i, u, back=2)
                    wait_group(act, S0["trans"], i, u)
                    nc.scalar.activation(edgeT[:, u % 2, :], ps_t[u % 2][:, :], ACT.Copy).then_inc(S0["edgeT"], 1)
                    wait_group(act, S0["msgp"], i, u, back=2)
                    wait_group(act, S0["pre"], i, u)
                    nc.scalar.activation(hT[:, u % 2, :], ps_h[u % 2][:, :], ACT.Relu, bias=b1_sb[:, :]).then_inc(S0["h"], 1)

            def steps1(i):
                for u in range(UNROLL):
                    wait_group(act, S1["seg"], i, u, back=2)
                    wait_group(act, S1["sum"], i, u)
                    nc.scalar.activation(msg[:, u % 2, :, :], pre1[:, u % 2, :, :], ACT.Relu).then_inc(S1["msg"], 1)

            def norm(S, in_psum):
                for c in range(CHUNKS + 1):
                    if c < CHUNKS:
                        if c >= 2:
                            act.wait_ge(S["var"], c - 1)
                        if in_psum:
                            act.wait_ge(S["nodes"], c + 1)
                            centred = ps_nodes[c % NBANKS][0:NP, 0:CB * D].rearrange("p (k f) -> p k f", f=D)
                        else:
                            act.wait_ge(S["resid"], c + 1)
                            centred = resid[:, c * CB:(c + 1) * CB, :]
                        nc.scalar.activation(square[:, c % 2, :, :], centred, ACT.Square).then_inc(S["square"], 1)
                    if c >= 1:
                        b = c - 1
                        act.wait_ge(S["var"], b + 1)
                        nc.scalar.activation(std[:, b * CB:(b + 1) * CB], var[:, b * CB:(b + 1) * CB], ACT.Sqrt,
                                             bias=norm_eps[0:NP, :], scale=1.0 / D).then_inc(S["std"], 1)

            def windowed():
                peeled(act, steps0)
                norm(S0, in_psum=True)
                peeled(act, steps1)
                norm(S1, in_psum=False)

            def general_steps0(h):
                for u in range(2):
                    wait_count(act, G0["trans"], h, 2, u + 1)
                    nc.scalar.activation(edgeT[:, 0, :], ps_t[0][:, :], ACT.Copy).then_inc(G0["edgeT"], 1)
                    wait_count(act, G0["pre"], h, 2, u + 1)
                    nc.scalar.activation(hT[:, 0, :], ps_h[0][:, :], ACT.Relu, bias=b1_sb[:, :]).then_inc(G0["h"], 1)

            def general_steps1(h):
                for u in range(2):
                    wait_count(act, G1["sum"], h, 2, u + 1)
                    nc.scalar.activation(msg[:, 0, :, :], pre1[:, 0, :, :], ACT.Relu).then_inc(G1["msg"], 1)

            def general():
                peeled(act, general_steps0, HALVES)
                norm(S0, in_psum=False)
                peeled(act, general_steps1, HALVES)
                norm(S1, in_psum=False)

            act.wait_ge(s_set, 1)
            by_width(act, general, windowed)

        @block.tensor
        def _(pe):
            pe.wait_ge(s_set, 1)
            pe.wait_ge(s_spread, 1)
            nc.tensor.matmul(ps_t[0][:, 0:GROUPS], lhsT=ones[:, :], rhs=spread[:, :, :].rearrange("p q c -> p (q c)"),
                             start=True, stop=True).then_inc(s_windows, 1)
            pe.wait_ge(s_wide, 1)
            nc.tensor.matmul(ps_t[1][:, 0:4], lhsT=ones[:, :], rhs=wide[:, :], start=True, stop=True).then_inc(s_n_wide, 1)
            pe.wait_ge(s_ident, 16)
            pe.wait_ge(s_const, 16 * N_CONST)

            def sum_messages(S, i, u, back):
                wait_group(pe, S["acc"], i, u, back=back + 1)
                wait_group(pe, S["msg"], i, u, back=back)
                v = (u - back) % UNROLL
                for t in range(TILES):
                    last = nc.tensor.matmul(ps_s[:, :], lhsT=msg[:, v % 2, t, :], rhs=edge[:, v, t, 0:WIN],
                                            start=(t == 0), stop=(t == TILES - 1))
                last.then_inc(S["seg"], 1)

            def output_layer(i, u, back):
                v = (u - back) % UNROLL
                wait_group(pe, S0["msg"], i, u, back=back + 1)
                wait_group(pe, S0["h"], i, u, back=back)
                for t in range(TILES):
                    last = nc.tensor.matmul(ps_m[:, t, :], lhsT=hT[:, v % 2, t * P:(t + 1) * P], rhs=w2_sb[:, :],
                                            start=True, stop=True)
                last.then_inc(S0["msgp"], 1)

            def steps0(i):
                for u in range(UNROLL):
                    pe.wait_ge(S0["window"][u], i * 16 + 16)
                    wait_group(pe, S0["stat"], i, u, back=1)
                    pe.wait_ge(S0["edges"][u // 2], i * 16 + 16)
                    wait_group(pe, S0["onehot"], i, u)
                    wait_group(pe, S0["edgeT"], i, u, back=2)
                    pe.wait_ge(S0["rows"][u], i * (16 * TILES) + 16 * TILES)
                    for t in range(TILES):
                        last = nc.tensor.transpose(ps_t[u % 2][:, t * P:(t + 1) * P], edge[:, u, t, :], ident_sb[:, :])
                    last.then_inc(S0["trans"], 1)
                    nc.tensor.matmul(ps_a[:, :], lhsT=x_win[:, u, :], rhs=w1_dst[:, :], start=True, stop=True).then_inc(S0["awin"], 1)
                    if not first_group(i, u):
                        output_layer(i, u, 1)
                    wait_group(pe, S0["stat"], i, u)
                    wait_group(pe, S0["h"], i, u, back=2)
                    wait_group(pe, S0["edgeT"], i, u)
                    nc.tensor.matmul(ps_h[u % 2][:, :], lhsT=w_edge[:, u, :], rhs=edgeT[:, u % 2, :], start=True, stop=True).then_inc(S0["pre"], 1)
                    if not first_group(i, u):
                        sum_messages(S0, i, u, 1)

            def steps1(i):
                for u in range(UNROLL):
                    wait_group(pe, S1["onehot"], i, u)
                    sum_messages(S1, i, u, 0)

            def to_nodes(S, n, freed):
                pe.wait_ge(S["acc"], GROUPS)
                for c in range(CHUNKS):
                    if c >= NBANKS:
                        pe.wait_ge(S[freed], c - NBANKS + 1)
                    for k in range(CB):
                        first = c * CB + k
                        last = nc.tensor.matmul(ps_nodes[c % NBANKS][0:NP, k * D:(k + 1) * D],
                                                lhsT=acc[n][0:D, first:first + (NP - 1) * BLK + 1:BLK],
                                                rhs=center_sb[:, :], start=True, stop=True)
                    last.then_inc(S["nodes"], 1)

            def windowed():
                peeled(pe, steps0)
                output_layer(ITERS, 0, 1)
                sum_messages(S0, ITERS, 0, 1)
                to_nodes(S0, 0, "norm")
                peeled(pe, steps1)
                to_nodes(S1, 1, "resid")

            def merge_tiles(G, h, u):
                for t in range(TILES):
                    n = u * TILES + t
                    wait_count(pe, G["dst"], h, 2, u + 1)
                    wait_count(pe, G["same"], h, 2 * TILES, n)
                    nc.tensor.transpose(ps_row, dst_f[:, t:t + 1].to_broadcast([P, P]), ident_sb[:, :]).then_inc(G["row"], 1)
                    wait_count(pe, G["addend"], h, 2 * TILES, n)
                    wait_count(pe, G["msg"], h, 2, u + 1)
                    wait_count(pe, G["same"], h, 2 * TILES, n + 1)
                    nc.tensor.matmul(ps_merged, lhsT=same[:, :], rhs=msg[:, 0, t, :], start=True, stop=True).then_inc(G["merged"], 1)

            def general_steps0(h):
                for u in range(2):
                    pe.wait_ge(G0["edges"], h * 16 + 16)
                    wait_count(pe, G0["rows"], h, 64 * TILES, (u + 1) * 32 * TILES)
                    for t in range(TILES):
                        last = nc.tensor.transpose(ps_t[0][:, t * P:(t + 1) * P], edge[:, u, t, :], ident_sb[:, :])
                    last.then_inc(G0["trans"], 1)
                    wait_count(pe, G0["edgeT"], h, 2, u + 1)
                    nc.tensor.matmul(ps_h[0][:, :], lhsT=w_full[:, :], rhs=edgeT[:, 0, :], start=True, stop=True).then_inc(G0["pre"], 1)
                    wait_count(pe, G0["h"], h, 2, u + 1)
                    for t in range(TILES):
                        last = nc.tensor.matmul(ps_m[:, t, :], lhsT=hT[:, 0, t * P:(t + 1) * P], rhs=w2_sb[:, :], start=True, stop=True)
                    last.then_inc(G0["msgp"], 1)
                    merge_tiles(G0, h, u)

            def general_steps1(h):
                for u in range(2):
                    merge_tiles(G1, h, u)

            def general():
                pe.wait_ge(s_known, 2)
                peeled(pe, general_steps0, HALVES)
                peeled(pe, general_steps1, HALVES)

            by_width(pe, general, windowed)

        @block.vector
        def _(dve):
            def linked(s):
                count = [0]

                def link(ins):
                    count[0] += 1
                    ins.then_inc(s, 1)
                    dve.wait_ge(s, count[0])
                return link

            link = linked(s_prologue)
            nc.vector.memset(zeros[:, :], 0.0)
            nc.vector.memset(norm_eps[:, :], NORM_EPS)
            nc.vector.memset(rel[:, GROUPS:GROUPS + 1, :], -1.0)
            link(nc.vector.memset(ones[:, :], 1.0))
            dve.sem_inc(s_set, 1)
            dve.wait_ge(s_dst_g, 16)
            by_group = dst_g.rearrange("p (g e) -> p g e", g=4)
            link(nc.vector.tensor_reduce(low[:, :], by_group, AX.X, ALU.min))
            link(nc.vector.tensor_scalar(base[:, :], low[:, :], float(N - WIN), None, ALU.min))
            dve.wait_ge(s_ident, 16)
            nc.vector.tensor_tensor(spread[:, :, :], ident_sb[0:GP, 0:GP].unsqueeze(2).to_broadcast([GP, GP, 4]),
                                    base[:, :].unsqueeze(1).to_broadcast([GP, GP, 4]), ALU.mult).then_inc(s_spread, 1)
            link(nc.vector.tensor_reduce(high[:, :], by_group, AX.X, ALU.max))
            link(nc.vector.tensor_tensor(high[:, :], high[:, :], base[:, :], ALU.subtract))
            nc.vector.tensor_scalar(wide[:, :], high[:, :], float(WIN), None, ALU.is_ge).then_inc(s_wide, 1)
            dve.wait_ge(s_windows, 1)
            nc.vector.tensor_copy(base_row[:, :], ps_t[0][0:1, 0:GROUPS]).then_inc(s_known, 1)
            dve.wait_ge(s_n_wide, 1)
            link(nc.vector.tensor_reduce(n_wide[:, :], ps_t[1][0:1, 0:4], AX.X, ALU.add))
            nc.vector.tensor_copy(n_wide_i[:, :], n_wide[:, :]).then_inc(s_known, 1)
            dve.wait_ge(s_dst_t, 16)
            link(nc.vector.tensor_tensor(rel[:, 0:GROUPS, :], dst_t.rearrange("p (g t) -> p g t", t=TILES),
                                         ps_t[0][:, 0:GROUPS].unsqueeze(2).to_broadcast([P, GROUPS, TILES]), ALU.subtract))
            dve.wait_ge(s_const, 16 * N_CONST)
            link(nc.vector.tensor_scalar(res_scale[:, :], res_scale[:, :], 2.0, None, ALU.add))

            def onehot(S, i, u, ahead=0):
                wait_group(dve, S["seg"], i, u, back=UNROLL - ahead)
                for t in range(TILES):
                    last = nc.vector.tensor_scalar(edge[:, (u + ahead) % UNROLL, t, 0:WIN], iota_sb[:, :],
                                                   rel[:, bass.ds(i * UNROLL + u + ahead, 1), t], None, ALU.is_equal)
                last.then_inc(S["onehot"], 1)

            def accumulate(S, n, i, u, back):
                first = dve.value_load(base_row[0:1, bass.ds(i * UNROLL + (u - back), 1)], min_val=0, max_val=N - WIN)
                wait_group(dve, S["acc"], i, u, back=back + 1)
                wait_group(dve, S["seg"], i, u, back=back)
                nc.vector.tensor_tensor(acc[n][0:D, bass.ds(first, WIN)], acc[n][0:D, bass.ds(first, WIN)], ps_s[:, :], ALU.add).then_inc(S["acc"], 1)

            def add_b2(done, slot):
                nc.vector.tensor_tensor(msg[:, slot, :, :], ps_m[:, :, :], b2_sb[:, :].unsqueeze(1).to_broadcast([P, TILES, D]),
                                        ALU.add).then_inc(done, 1)

            def offset_messages(i, u, back):
                wait_group(dve, S0["seg"], i, u, back=back + 2)
                wait_group(dve, S0["msgp"], i, u, back=back)
                add_b2(S0["msg"], (u - back) % 2)

            def steps0(i):
                nc.vector.tensor_copy(acc[1][0:D, bass.ds(i * P, P)], zeros[:, :])
                for u in range(UNROLL):
                    wait_group(dve, S0["pre"], i, u, back=UNROLL)
                    wait_group(dve, S0["awin"], i, u)
                    nc.vector.tensor_copy(w_edge[0:WIN, u, :], ps_a[:, :]).then_inc(S0["stat"], 1)
                    onehot(S0, i, u, ahead=1)
                    if not first_group(i, u):
                        offset_messages(i, u, 1)
                        accumulate(S0, 0, i, u, 1)

            def steps1(i):
                for u in range(UNROLL):
                    onehot(S1, i, u, ahead=1)
                    wait_group(dve, S1["msg"], i, u, back=2)
                    dve.wait_ge(S1["edges"][u // 2], i * 16 + 16)
                    dve.wait_ge(S1["rows"][u], i * (16 * TILES) + 16 * TILES)
                    nc.vector.tensor_tensor(pre1[:, u % 2, :, :], edge[:, u, :, D:2 * D], e48_sb[:, u, :, :], ALU.add).then_inc(S1["sum"], 1)
                    if not first_group(i, u):
                        accumulate(S1, 1, i, u, 1)

            def chunk(t, c):
                return t[:, c * CB:(c + 1) * CB]

            def over_features(t):
                return t.unsqueeze(2).to_broadcast([NP, CB, D])

            def norm(S, link, center, in_psum):
                for c in range(CHUNKS + 1):
                    if c < CHUNKS:
                        center(c)
                        dve.wait_ge(S["square"], c + 1)
                        nc.vector.tensor_reduce(chunk(var, c), square[:, c % 2, :, :], AX.X, ALU.add).then_inc(S["var"], 1)
                    if c >= 1:
                        b = c - 1
                        centred = (ps_nodes[b % NBANKS][0:NP, 0:CB * D].rearrange("p (k f) -> p k f", f=D) if in_psum
                                   else resid[:, b * CB:(b + 1) * CB, :])
                        dve.wait_ge(S["std"], b + 1)
                        link(nc.vector.reciprocal(chunk(rstd, b), chunk(std, b)))
                        nc.vector.tensor_tensor(feats[:, b * CB:(b + 1) * CB, :], centred, over_features(chunk(rstd, b)), ALU.mult).then_inc(S["norm"], 1)

            def windowed():
                link = linked(s_narrow)

                def center1(c):
                    dve.wait_ge(S1["nodes"], c + 1)
                    summed = ps_nodes[c % NBANKS][0:NP, 0:CB * D].rearrange("p (k f) -> p k f", f=D)
                    nc.vector.scalar_tensor_tensor(resid[:, c * CB:(c + 1) * CB, :], feats[:, c * CB:(c + 1) * CB, :],
                                                   res_scale[0:NP, :], summed, ALU.mult, ALU.add).then_inc(S1["resid"], 1)

                onehot(S0, 0, 0)
                dve.wait_ge(s_xT, 16)
                peeled(dve, steps0)
                offset_messages(ITERS, 0, 1)
                accumulate(S0, 0, ITERS, 0, 1)
                onehot(S1, 0, 0)
                norm(S0, link, lambda c: None, in_psum=True)
                peeled(dve, steps1)
                accumulate(S1, 1, ITERS, 0, 1)
                dve.wait_ge(s_x1, 16 * CHUNKS)
                norm(S1, link, center1, in_psum=False)

            def general_layer(G, S, n, link):
                per_half = [0]

                def steps(h):
                    count = [0]

                    def step(ins):
                        count[0] += 1
                        ins.then_inc(G["step"], 1)
                        wait_count(dve, G["step"], h, per_half[0], count[0])

                    for u in range(2):
                        dst_of = dst_t[:, bass.ds(h * (2 * TILES) + u * TILES, TILES)]
                        if n == 0:
                            step(nc.vector.tensor_scalar(dst_idx[:, :], dst_of, 0.0, None, ALU.add))
                        nc.vector.tensor_scalar(dst_f[:, :], dst_of, 0.0, None, ALU.add).then_inc(G["dst"], 1)
                        if n == 0:
                            wait_count(dve, G["msgp"], h, 2, u + 1)
                            add_b2(G["msg"], 0)
                        else:
                            dve.wait_ge(G["edges"], h * 16 + 16)
                            wait_count(dve, G["rows"], h, 32 * TILES, (u + 1) * 16 * TILES)
                            nc.vector.tensor_tensor(pre1[:, 0, :, :], edge[:, u, :, D:2 * D], e48_sb[:, u, :, :], ALU.add).then_inc(G["sum"], 1)
                        for t in range(TILES):
                            m = u * TILES + t
                            wait_count(dve, G["dst"], h, 2, u + 1)
                            wait_count(dve, G["row"], h, 2 * TILES, m + 1)
                            nc.vector.tensor_scalar(same[:, :], ps_row, dst_f[:, t:t + 1], None, ALU.is_equal).then_inc(G["same"], 1)
                            wait_count(dve, G["same"], h, 2 * TILES, m + 1)
                            step(nc.vector.tensor_tensor(same_earlier[:, :], same[:, :], earlier_sb[:, :], ALU.mult))
                            step(nc.vector.tensor_reduce(n_earlier[:, :], same_earlier[:, :], AX.X, ALU.add))
                            step(nc.vector.tensor_tensor(to_spare[:, :], spare_sb[:, :], dst_f[:, t:t + 1], ALU.subtract))
                            step(nc.vector.scalar_tensor_tensor(to_spare[:, :], n_earlier[:, :], 0.0, to_spare[:, :], ALU.is_gt, ALU.mult))
                            wait_count(dve, G["added"], h, 32 * TILES, 16 * m)
                            step(nc.vector.tensor_tensor(target[:, :], to_spare[:, :], dst_f[:, t:t + 1], ALU.add))
                            wait_count(dve, G["merged"], h, 2 * TILES, m + 1)
                            nc.vector.tensor_copy(addend[:, :], ps_merged).then_inc(G["addend"], 1)
                    per_half[0] = count[0]

                def center(c):
                    r, f = resid[:, c * CB:(c + 1) * CB, :], feats[:, c * CB:(c + 1) * CB, :]
                    if n == 0:
                        link(nc.vector.tensor_tensor(r, r, f, ALU.add))
                    else:
                        link(nc.vector.scalar_tensor_tensor(r, f, res_scale[0:NP, :], r, ALU.mult, ALU.add))
                    link(nc.vector.tensor_reduce(chunk(mean, c), r, AX.X, ALU.add))
                    link(nc.vector.tensor_scalar(chunk(mean, c), chunk(mean, c), 1.0 / D, None, ALU.mult))
                    nc.vector.tensor_tensor(r, r, over_features(chunk(mean, c)), ALU.subtract).then_inc(S["resid"], 1)

                nc.vector.memset(zero_table, 0.0).then_inc(G["zeroed"], 1)
                peeled(dve, steps, HALVES)
                dve.wait_ge(G["table"], 32)
                norm(S, link, center, in_psum=False)

            def general():
                link = linked(s_general)
                dve.wait_ge(s_x, 16)
                dve.wait_ge(s_xT, 16)
                general_layer(G0, S0, 0, link)
                dve.wait_ge(s_x1, 16 * CHUNKS)
                general_layer(G1, S1, 1, link)

            by_width(dve, general, windowed)


def kernel(**inputs):
    import numpy as np
    import concourse.bacc as bacc
    from concourse.bass_utils import run_bass_kernel_spmd

    x, src, dst = (np.asarray(inputs[k]) for k in ("x", "src", "dst"))
    e32, e48 = np.asarray(inputs["edge_attr_32"]), np.asarray(inputs["edge_attr_48"])

    def padded_rows(a, rows, fill):
        out = np.full((rows,) + a.shape[1:], fill, a.dtype)
        out[:a.shape[0]] = a
        return out

    def by_halves(a):
        f = a.shape[1]
        a = padded_rows(a, EPAD, 0).reshape(HALVES, 2, P, TILES * f)
        return np.ascontiguousarray(a.transpose(0, 2, 1, 3)).reshape(HALVES, P, 2 * TILES * f)

    def by_tiles(a, fill):
        a = padded_rows(a, EPAD, fill).reshape(GROUPS, P, TILES)
        return np.ascontiguousarray(a.transpose(1, 0, 2)).reshape(P, GROUPS * TILES)

    arrays = {
        "x": padded_rows(x, XROWS, 0),
        "xT": np.ascontiguousarray(x.T),
        "src_tiles": by_tiles(src, 0).view(np.uint32),
        "dst_tiles": by_tiles(dst, N),
        "dst_groups": padded_rows(dst, EPAD, dst[-1]).reshape(GP, 4 * GE),
        "e32": by_halves(e32),
        "e48": by_halves(e48),
        "w1": np.asarray(inputs["L0_gnn_W1"]),
        "w2": np.asarray(inputs["L0_gnn_W2"]),
        "b1": np.asarray(inputs["L0_gnn_b1"]).reshape(H, 1),
        "b2": np.asarray(inputs["L0_gnn_b2"]).reshape(1, D),
        "eps": np.asarray(inputs["L1_gnn_eps"]).reshape(1, 1),
        "ident": np.eye(P, dtype=np.float32),
        "iota": np.tile(np.arange(WIN, dtype=np.float32), (P, 1)),
        "center": (np.eye(D) - 1.0 / D).astype(np.float32),
        "earlier": np.tril(np.ones((P, P), np.float32), -1),
        "spare": (N + 1 + np.arange(P, dtype=np.float32)).reshape(P, 1),
    }
    nc = bacc.Bacc("TRN2", target_bir_lowering=False, num_devices=1)
    args = [nc.dram_tensor(k, a.shape, mybir.dt.from_np(a.dtype), kind="ExternalInput").ap() for k, a in arrays.items()]
    out = nc.dram_tensor("out", (N, D), F32, kind="ExternalOutput").ap()
    build(nc, *args, out)
    return run_bass_kernel_spmd(nc, [arrays], core_ids=[0]).results[0]["out"]
```

```python
from contextlib import ExitStack

import concourse.bass as bass
from concourse import mybir

F32 = mybir.dt.float32
I32 = mybir.dt.int32
U32 = mybir.dt.uint32
ALU = mybir.AluOpType
ACT = mybir.ActivationFunctionType
AX = mybir.AxisListType

N = 12500
D = 48
DE = 32
H = 128
E = 200000
P = 128
TILES = 4
GE = P * TILES
UNROLL = 4
WIN = 48
GROUPS = -(-E // GE)
ITERS = -(-GROUPS // UNROLL)
LAST = GROUPS - 1 - (ITERS - 1) * UNROLL
SLOTS = ITERS * UNROLL
EPAD = SLOTS * GE
HALVES = SLOTS // 2
CHUNKS = 10
CN = N // CHUNKS
CB = 10
NP = CN // CB
PICK = UNROLL - 1
EARLY = CHUNKS - 1
NORM_ITER = ITERS - 1 - EARLY
ACCW = P * ITERS
XROWS = N + 1
TROWS = -(-(XROWS + P) // P) * P
NORM_EPS = 1e-5
HALF = CHUNKS // 2
SHARES = (range(0, 2), range(2, HALF), range(HALF, 8), range(8, CHUNKS))
ROUND = 1.5 * 2 ** 23
assert CHUNKS * NP * CB == N and NP <= P and ACCW >= N and ITERS <= P and CB * D <= GE and WIN + D + DE == P
assert UNROLL * GE + SLOTS * TILES + TROWS // P * D <= ACCW


def build(nc, x, xT, src_tiles, dst_tiles, dst_groups, e32, e48, w1, w2, b1, b2, eps, ident, iota, center, normed, src_rows, src_columns, places,
          earlier, spare, out):
    ctx = ExitStack()
    with ctx:
        def sb(name, shape, dt=F32):
            return ctx.enter_context(nc.sbuf_tensor(name, shape, dt))

        def pb(name, shape, dt=F32):
            return ctx.enter_context(nc.psum_tensor(name, shape, dt))

        def sem(name):
            return ctx.enter_context(nc.semaphore(name))

        def sems(name, n):
            return [sem(f"{name}{k}") for k in range(n)]

        x1_dram = nc.dram_tensor("x1_dram", (N, D), F32, kind="Internal").ap()
        table = [nc.dram_tensor(f"table{n}_dram", (TROWS, D), F32, kind="Internal").ap() for n in range(2)]

        ident_sb = sb("ident_sb", [P, P])
        iota_sb = sb("iota_sb", [P, WIN])
        center_sb = sb("center_sb", [D, D])
        w1_dst = sb("w1_dst", [D, H])
        w2_sb = sb("w2_sb", [H, D])
        b1_sb = sb("b1_sb", [H, 1])
        b2_sb = sb("b2_sb", [P, D])
        res_scale = sb("res_scale", [P, 1])
        norm_eps = sb("norm_eps", [P, 1])
        zeros = sb("zeros", [D, P])
        ones = sb("ones", [ITERS, P])
        low = sb("low", [ITERS, UNROLL])
        high = sb("high", [ITERS, UNROLL])
        base = sb("base", [ITERS, UNROLL])
        wide = sb("wide", [ITERS, UNROLL])
        normed_sb = sb("normed_sb", [ITERS, 1])
        late = sb("late", [ITERS, UNROLL])
        spread = sb("spread", [ITERS, ITERS, UNROLL])
        base_row = sb("base_row", [1, SLOTS], I32)
        n_wide = sb("n_wide", [1, 1])
        n_wide_i = sb("n_wide_i", [1, 1], I32)
        rel = sb("rel", [P, SLOTS, TILES])
        idx = sb("idx", [P, UNROLL, TILES], U32)
        edge = sb("edge", [P, UNROLL, TILES, P])
        e48_sb = sb("e48_sb", [P, UNROLL, TILES, D])
        x_win = sb("x_win", [D, UNROLL, WIN])
        w_edge = sb("w_edge", [P, UNROLL, H])
        edgeT = sb("edgeT", [P, 2, GE])
        hT = sb("hT", [H, 2, GE])
        pre1 = sb("pre1", [P, 2, TILES, D])
        msg = sb("msg", [P, 2, TILES, D])
        src_row = sb("src_row", [NP, P], I32)
        first_rows = sb("first_rows", [NP, 2, P], I32)
        row_place = sb("row_place", [NP, P])
        places_sb = sb("places_sb", [NP, CHUNKS])
        at_place = sb("at_place", [NP, CHUNKS, P])
        src_col = sb("src_col", [P, ITERS], I32)
        col_place = sb("col_place", [P, ITERS])
        col_rest = sb("col_rest", [P, ITERS])
        picked = sb("picked", [P, CB, D])
        acc = [sb("acc0", [D, ACCW]), sb("acc1", [P, ACCW])]
        dst_g = acc[1][0:ITERS, 0:UNROLL * GE].bitcast(I32)
        dst_t = acc[1][:, UNROLL * GE:UNROLL * GE + SLOTS * TILES].bitcast(I32)
        zero_table = acc[1][:, UNROLL * GE + SLOTS * TILES:UNROLL * GE + SLOTS * TILES + TROWS // P * D]
        staged = sb("staged", [D, CN])
        feats = sb("feats", [NP, CHUNKS, CB * D])
        resid = sb("resid", [NP, CHUNKS, CB * D])
        square = sb("square", [NP, 2, CB * D])
        mean = sb("mean", [NP, CHUNKS, CB])
        var = sb("var", [NP, CHUNKS, CB])
        std = sb("std", [NP, CHUNKS, CB])
        rstd = sb("rstd", [NP, CHUNKS, CB])
        dst_idx = sb("dst_idx", [P, TILES], U32)
        dst_f = sb("dst_f", [P, TILES])
        w_full = sb("w_full", [P, H])
        earlier_sb = sb("earlier_sb", [P, P])
        spare_sb = sb("spare_sb", [P, 1])
        same = sb("same", [P, P])
        same_earlier = sb("same_earlier", [P, P])
        n_earlier = sb("n_earlier", [P, 1])
        to_spare = sb("to_spare", [P, 1])
        target = sb("target", [P, 1], U32)
        addend = sb("addend", [P, D])

        ps_t = [pb(f"ps_t{k}", [P, GE]) for k in range(2)]
        ps_h = [pb(f"ps_h{k}", [H, GE]) for k in range(2)]
        ps_a = pb("ps_a", [WIN, H])
        ps_m = pb("ps_m", [P, TILES, D])
        ps_s = pb("ps_s", [D, WIN])
        ps_nodes = pb("ps_nodes", [P, GE])[0:NP, 0:CB * D]
        ps_picked = ps_h[0][:, 0:CB * D]
        ps_row, ps_merged = ps_t[1][:, 0:P], ps_h[1][:, 0:D]

        s_dst_g = sem("s_dst_g")
        s_dst_t = sem("s_dst_t")
        s_ident = sem("s_ident")
        s_normed = sem("s_normed")
        s_const = sem("s_const")
        s_set = sem("s_set")
        s_spread = sem("s_spread")
        s_wide = sem("s_wide")
        s_windows = sem("s_windows")
        s_n_wide = sem("s_n_wide")
        s_known = sem("s_known")
        s_prologue = sem("s_prologue")
        s_general = sem("s_general")
        s_passed = sem("s_passed")
        s_xT = sem("s_xT")
        s_x = sem("s_x")
        s_x1 = sem("s_x1")
        s_out = sem("s_out")
        N_CONST = 18

        def layer_sems(n):
            per_slot = {"idx": 2, "edges": 2, "window": UNROLL, "rows": UNROLL}
            counts = ("onehot", "awin", "stat", "trans", "edgeT", "pre", "h", "msgp", "sum", "msg", "seg", "acc",
                      "src_row", "place", "places_a", "places_b", "rest", "half", "ten", "picked", "staged", "nodes", "resid", "square", "var", "std", "rstd", "norm")
            return {**{w: sems(f"s{n}_{w}", k) for w, k in per_slot.items()}, **{w: sem(f"s{n}_{w}") for w in counts}}

        def general_sems(n):
            counts = ("zeroed", "table", "idx", "edges", "dst", "rows", "trans", "edgeT", "pre", "h", "msgp", "sum",
                      "msg", "row", "same", "merged", "addend", "added", "step")
            return {w: sem(f"g{n}_{w}") for w in counts}

        S0, S1 = layer_sems(0), layer_sems(1)
        G0, G1 = general_sems(0), general_sems(1)
        block = ctx.enter_context(nc.Block())

        def wait_group(eng, s, i, u, back=0):
            if isinstance(i, int) and UNROLL * i + u - back < 0:
                return
            eng.wait_ge(s, i * UNROLL + (u - back + 1))

        def wait_count(eng, s, h, per, n):
            if isinstance(h, int) and per * h + n <= 0:
                return
            eng.wait_ge(s, h * per + n)

        def peeled(eng, body, count):
            body(0)
            with eng.Fori(1, count) as i:
                body(i)

        def layer(eng, body):
            body(0, None)
            with eng.Fori(1, NORM_ITER) as i:
                body(i, None)
            with eng.Fori(NORM_ITER, ITERS - 1) as i:
                body(i, i - NORM_ITER)
            body(ITERS - 1, None)

        def gathered(S, u):
            return TILES - 1 if S is S1 and u == PICK else TILES

        def groups_of(i):
            return range(LAST + 1 if last_iteration(i) else UNROLL)

        def first_iteration(i):
            return isinstance(i, int) and i == 0

        def last_iteration(i):
            return isinstance(i, int) and i == ITERS - 1

        def first_group(i, u):
            return first_iteration(i) and u == 0

        def last_group(i, u):
            return last_iteration(i) and u == LAST

        def by_width(eng, general, windowed):
            eng.wait_ge(s_known, 2)
            wide_groups = eng.value_load(n_wide_i[0:1, 0:1], min_val=0, max_val=SLOTS)
            with eng.If(wide_groups > 0):
                general()
            with eng.Else():
                windowed()

        def one(t, c):
            return t[:, bass.ds(c, 1)]

        def by_chunk(sums):
            return sums[0:D, 0:N].rearrange("d (c n) -> d c n", c=CHUNKS)

        def by_node(dram):
            return dram.rearrange("(c p k) f -> p c (k f)", c=CHUNKS, p=NP)

        def store_chunk(sp, n, c):
            S, dram, nodes, done = ((S0, x1_dram, feats, s_x1), (S1, out, resid, s_out))[n]
            sp.wait_ge(S["norm"], c + 1)
            sp.dma_start(one(by_node(dram), c), one(nodes, c)).then_inc(done, 16)

        @block.sync
        def _(sp):
            def load_idx(done, i, h, slot):
                sp.dma_start(idx[:, slot:slot + 2, :].rearrange("p g t -> p (g t)"),
                             src_tiles[:, bass.ds(i * (UNROLL * TILES) + h * 2 * TILES, 2 * TILES)]).then_inc(done, 16)

            def load_e32(done, half, slot):
                sp.dma_start(edge[:, slot:slot + 2, :, 2 * D:P].rearrange("p g t f -> p (g t) f"),
                             e32[bass.ds(half, 1), :, :].rearrange("a p (t f) -> (a p) t f", f=DE)).then_inc(done, 16)

            def load_e48(done, half, slot):
                sp.dma_start(e48_sb[:, slot:slot + 2, :, :].rearrange("p g t f -> p (g t f)"),
                             e48[bass.ds(half, 1), :, :].rearrange("a p n -> (a p) n")).then_inc(done, 16)

            load_idx(S0["idx"][0], 0, 0, 0)
            sp.dma_start(dst_g, dst_groups).then_inc(s_dst_g, 16)
            load_idx(S0["idx"][1], 0, 1, 2)
            sp.dma_start(dst_t, dst_tiles).then_inc(s_dst_t, 16)

            def loads0(i, c):
                for u in groups_of(i):
                    if u % 2 == 0:
                        wait_group(sp, S0["trans"], i, u + 1, back=UNROLL)
                        if not first_iteration(i):
                            load_idx(S0["idx"][u // 2], i, u // 2, u)
                        load_e32(S0["edges"][u // 2], i * 2 + u // 2, u)
                    wait_group(sp, S0["awin"], i, u, back=UNROLL)
                    first = sp.value_load(base_row[0:1, bass.ds(i * UNROLL + u, 1)], min_val=0, max_val=N - WIN)
                    sp.dma_start(x_win[:, u, :], xT[:, bass.ds(first, WIN)]).then_inc(S0["window"][u], 16)

                if c is not None:
                    store_chunk(sp, 0, c)

            def loads1(i, c):
                for h in range(2):
                    wait_group(sp, S1["sum"], i, 2 * h + 1, back=UNROLL)
                    load_idx(S1["idx"][h], i, h, 2 * h)
                    load_e48(S1["edges"][h], i * 2 + h, 2 * h)
                    if h == PICK // 2 and not last_iteration(i):
                        sp.dma_start(src_row[:, :], src_rows[bass.ds(i + 2, 1), :].to_broadcast([NP, P])).then_inc(S1["src_row"], 16)
                if c is not None:
                    store_chunk(sp, 1, c)

            def loads_and_stores(loads):
                with sp.Fori(1, NORM_ITER + 1) as i:
                    loads(i, None)
                with sp.Fori(NORM_ITER + 1, ITERS - 1) as i:
                    loads(i, i - (NORM_ITER + 1))
                loads(ITERS - 1, EARLY - 1)

            def windowed():
                loads0(0, None)
                loads_and_stores(loads0)
                sp.wait_ge(S0["trans"], GROUPS)
                loads1(0, None)
                store_chunk(sp, 0, EARLY)
                loads_and_stores(loads1)
                store_chunk(sp, 1, EARLY)
                sp.wait_ge(s_x1, 16 * CHUNKS)
                sp.wait_ge(s_out, 16 * CHUNKS)

            def general_layer(G, n):
                def loads(h):
                    wait_count(sp, G["added"], h, 32 * TILES, 0)
                    sp.dma_start(idx[:, 0:2, :].rearrange("p g t -> p (g t)"),
                                 src_tiles[:, bass.ds(h * 2 * TILES, 2 * TILES)]).then_inc(G["idx"], 16)
                    (load_e48 if n else load_e32)(G["edges"], h, 0)

                sp.wait_ge(G["zeroed"], 1)
                sp.dma_start(table[n].rearrange("(p r) f -> p (r f)", p=P), zero_table).then_inc(G["table"], 16)
                peeled(sp, loads, HALVES)
                sp.wait_ge(G["added"], 16 * TILES * SLOTS)
                sp.wait_ge(G["table"], 16)
                sp.dma_start(resid[:, :, :], by_node(table[n][0:N, :])).then_inc(G["table"], 16)

            def general():
                for u in range(UNROLL):
                    sp.wait_ge(S0["rows"][u], 16 * TILES)
                sp.dma_start(feats[:, :, :], by_node(x[0:N, :])).then_inc(s_x, 16)
                general_layer(G0, 0)
                for c in range(CHUNKS):
                    store_chunk(sp, 0, c)
                sp.wait_ge(s_x1, 16 * CHUNKS)
                general_layer(G1, 1)
                for c in range(CHUNKS):
                    store_chunk(sp, 1, c)
                sp.wait_ge(s_out, 16 * CHUNKS)

            by_width(sp, general, windowed)

        @block.gpsimd
        def _(pool):
            def gather(cols, rows_of, index, done):
                pool.indirect_dma_start(out=cols, out_offset=None, in_=rows_of,
                                        in_offset=bass.IndirectOffsetOnAxis(ap=index, axis=0)).then_inc(done, 16)

            def gathers(S, rows_of, read, i):
                for u in groups_of(i):
                    pool.wait_ge(S["idx"][u // 2], i * 16 + 16)
                    wait_group(pool, S[read], i, u, back=UNROLL)
                    pool.sem_inc(s_passed, 1)
                    for t in range(gathered(S, u)):
                        gather(edge[:, u, t, D:2 * D], rows_of, idx[:, u, t:t + 1], S["rows"][u])

            gathers(S0, x, "trans", 0)

            def windowed():
                def others(S, rows_of, read):
                    with pool.Fori(1, ITERS - 1) as i:
                        gathers(S, rows_of, read, i)
                    gathers(S, rows_of, read, ITERS - 1)

                others(S0, x, "trans")
                pool.wait_ge(s_x1, 16 * CHUNKS)
                gathers(S1, x1_dram, "sum", 0)
                others(S1, x1_dram, "sum")

            def general_layer(G, n):
                def steps(h):
                    for u in range(2):
                        pool.wait_ge(G["idx"], h * 16 + 16)
                        wait_count(pool, G["dst"], h, 2, u + 1)
                        pool.sem_inc(s_passed, 1)
                        for t in range(TILES):
                            gather(edge[:, u, t, D:2 * D], x1_dram if n else x, idx[:, u, t:t + 1], G["rows"])
                            if n == 0:
                                gather(edge[:, u, t, 0:D], x, dst_idx[:, t:t + 1], G["rows"])
                        for t in range(TILES):
                            wait_count(pool, G["addend"], h, 2 * TILES, u * TILES + t + 1)
                            pool.sem_inc(s_passed, 1)
                            pool.indirect_dma_start(out=table[n], in_=addend[:, :], in_offset=None, compute_op=ALU.add,
                                                    out_offset=bass.IndirectOffsetOnAxis(ap=target[:, :], axis=0),
                                                    ).then_inc(G["added"], 16)

                pool.wait_ge(G["table"], 16)
                peeled(pool, steps, HALVES)

            def general():
                for u in range(UNROLL):
                    pool.wait_ge(S0["rows"][u], 16 * TILES)
                general_layer(G0, 0)
                pool.wait_ge(s_x1, 16 * CHUNKS)
                general_layer(G1, 1)

            by_width(pool, general, windowed)

        @block.scalar
        def _(act):
            act.dma_start(ident_sb[:, :], ident).then_inc(s_ident, 16)
            act.dma_start(normed_sb[:, :], normed).then_inc(s_normed, 16)
            for dst, src in ((iota_sb[:, :], iota), (w1_dst[:, :], w1[0:D, :]), (w2_sb[:, :], w2), (b1_sb[:, :], b1),
                             (places_sb[:, :], places), (src_col[:, :], src_columns),
                             (first_rows[:, 0, :], src_rows[0:1, :].to_broadcast([NP, P])),
                             (first_rows[:, 1, :], src_rows[1:2, :].to_broadcast([NP, P])), (b2_sb[:, :], b2.to_broadcast([P, D])), (res_scale[:, :], eps.to_broadcast([P, 1])),
                             (center_sb[:, :], center), (w_full[:, :], w1), (earlier_sb[:, :], earlier), (spare_sb[:, :], spare)):
                act.dma_start(dst, src).then_inc(s_const, 16)
            for u in range(UNROLL):
                act.dma_start(w_edge[D:P, u, :], w1[D:P, :]).then_inc(s_const, 16)
            act.dma_start(acc[0][:, 0:N], xT).then_inc(s_xT, 16)
            act.wait_ge(s_const, 16 * N_CONST)

            def squares(S, slot, centred):
                nc.scalar.activation(square[:, slot:slot + 1, :], centred, ACT.Square).then_inc(S["square"], 1)

            def deviations(S, c):
                act.wait_ge(S["var"], c + 1)
                nc.scalar.activation(one(std, c), one(var, c), ACT.Sqrt, bias=norm_eps[0:NP, :], scale=1.0 / D).then_inc(S["std"], 1)

            def squares_of_sums(n, S, c):
                act.wait_ge(S["resid" if n else "nodes"], c + 1)
                squares(S, 0, one(resid, c) if n else ps_nodes.unsqueeze(1))

            def norm_steps_before(n, S, c, u):
                if c is not None and u == 2:
                    squares_of_sums(n, S, c)
                if c is not None and u == 3:
                    deviations(S, c)

            def norm_steps_after(n, S, i, c, u):
                if c is not None and u == 0:
                    act.wait_ge(S["acc"], i * UNROLL)
                    nc.scalar.activation(staged[:, :].unsqueeze(1), by_chunk(acc[n])[:, bass.ds(c, 1), :],
                                         ACT.Copy).then_inc(S["staged"], 1)

            def steps0(i, c):
                for u in groups_of(i):
                    norm_steps_before(0, S0, c, u)
                    wait_group(act, S0["pre"], i, u, back=2)
                    wait_group(act, S0["trans"], i, u)
                    nc.scalar.activation(edgeT[:, u % 2, :], ps_t[u % 2][:, :], ACT.Copy).then_inc(S0["edgeT"], 1)
                    wait_group(act, S0["msgp"], i, u, back=2)
                    wait_group(act, S0["pre"], i, u)
                    nc.scalar.activation(hT[:, u % 2, :], ps_h[u % 2][:, :], ACT.Relu, bias=b1_sb[:, :]).then_inc(S0["h"], 1)
                    norm_steps_after(0, S0, i, c, u)

            def steps1(i, c):
                for u in groups_of(i):
                    norm_steps_before(1, S1, c, u)
                    wait_group(act, S1["seg"], i, u, back=2)
                    wait_group(act, S1["sum"], i, u)
                    nc.scalar.activation(msg[:, u % 2, :, :], pre1[:, u % 2, :, :], ACT.Relu).then_inc(S1["msg"], 1)
                    norm_steps_after(1, S1, i, c, u)

            def windowed():
                for n, S, steps in ((0, S0, steps0), (1, S1, steps1)):
                    layer(act, steps)
                    squares_of_sums(n, S, EARLY)
                    deviations(S, EARLY)

            def norm(S):
                for c in range(CHUNKS + 1):
                    if c < CHUNKS:
                        if c >= 2:
                            act.wait_ge(S["var"], c - 1)
                        act.wait_ge(S["resid"], c + 1)
                        squares(S, c % 2, one(resid, c))
                    if c >= 1:
                        deviations(S, c - 1)

            def general_steps0(h):
                for u in range(2):
                    wait_count(act, G0["trans"], h, 2, u + 1)
                    nc.scalar.activation(edgeT[:, 0, :], ps_t[0][:, :], ACT.Copy).then_inc(G0["edgeT"], 1)
                    wait_count(act, G0["pre"], h, 2, u + 1)
                    nc.scalar.activation(hT[:, 0, :], ps_h[0][:, :], ACT.Relu, bias=b1_sb[:, :]).then_inc(G0["h"], 1)

            def general_steps1(h):
                for u in range(2):
                    wait_count(act, G1["sum"], h, 2, u + 1)
                    nc.scalar.activation(msg[:, 0, :, :], pre1[:, 0, :, :], ACT.Relu).then_inc(G1["msg"], 1)

            def general():
                peeled(act, general_steps0, HALVES)
                norm(S0)
                peeled(act, general_steps1, HALVES)
                norm(S1)

            act.wait_ge(s_set, 1)
            by_width(act, general, windowed)

        @block.tensor
        def _(pe):
            pe.wait_ge(s_set, 1)
            pe.wait_ge(s_spread, 1)
            nc.tensor.matmul(ps_t[0][:, 0:SLOTS], lhsT=ones[:, :], rhs=spread[:, :, :].rearrange("p q c -> p (q c)"),
                             start=True, stop=True).then_inc(s_windows, 1)
            pe.wait_ge(s_wide, 1)
            nc.tensor.matmul(ps_t[1][:, 0:UNROLL], lhsT=ones[:, :], rhs=wide[:, :], start=True, stop=True).then_inc(s_n_wide, 1)
            pe.wait_ge(s_ident, 16)
            pe.wait_ge(s_const, 16 * N_CONST)

            def sum_messages(S, i, u, back):
                wait_group(pe, S["acc"], i, u, back=back + 1)
                wait_group(pe, S["msg"], i, u, back=back)
                v = (u - back) % UNROLL
                for t in range(TILES):
                    last = nc.tensor.matmul(ps_s[:, :], lhsT=msg[:, v % 2, t, :], rhs=edge[:, v, t, 0:WIN],
                                            start=(t == 0), stop=(t == TILES - 1))
                last.then_inc(S["seg"], 1)

            def output_layer(i, u, back):
                v = (u - back) % UNROLL
                wait_group(pe, S0["msg"], i, u, back=back + 1)
                wait_group(pe, S0["h"], i, u, back=back)
                for t in range(TILES):
                    last = nc.tensor.matmul(ps_m[:, t, :], lhsT=hT[:, v % 2, t * P:(t + 1) * P], rhs=w2_sb[:, :],
                                            start=True, stop=True)
                last.then_inc(S0["msgp"], 1)

            def steps0(i, c):
                for u in groups_of(i):
                    pe.wait_ge(S0["window"][u], i * 16 + 16)
                    wait_group(pe, S0["stat"], i, u, back=1)
                    pe.wait_ge(S0["edges"][u // 2], i * 16 + 16)
                    wait_group(pe, S0["onehot"], i, u)
                    wait_group(pe, S0["edgeT"], i, u, back=2)
                    pe.wait_ge(S0["rows"][u], i * (16 * TILES) + 16 * TILES)
                    for t in range(TILES):
                        last = nc.tensor.transpose(ps_t[u % 2][:, t * P:(t + 1) * P], edge[:, u, t, :], ident_sb[:, :])
                    last.then_inc(S0["trans"], 1)
                    nc.tensor.matmul(ps_a[:, :], lhsT=x_win[:, u, :], rhs=w1_dst[:, :], start=True, stop=True).then_inc(S0["awin"], 1)
                    if not first_group(i, u):
                        output_layer(i, u, 1)
                    wait_group(pe, S0["stat"], i, u)
                    wait_group(pe, S0["h"], i, u, back=2)
                    wait_group(pe, S0["edgeT"], i, u)
                    nc.tensor.matmul(ps_h[u % 2][:, :], lhsT=w_edge[:, u, :], rhs=edgeT[:, u % 2, :], start=True, stop=True).then_inc(S0["pre"], 1)
                    if not first_group(i, u):
                        sum_messages(S0, i, u, 1)
                    if c is not None and u == 1:
                        pe.wait_ge(S0["staged"], c + 1)
                        to_nodes(S0, staged[:, :])

            def steps1(i, c):
                for u in groups_of(i):
                    wait_group(pe, S1["onehot"], i, u)
                    sum_messages(S1, i, u, 0)
                    if not last_iteration(i):
                        pick_rows(i + 1, SHARES[u])
                    if c is not None and u == 1:
                        pe.wait_ge(S1["staged"], c + 1)
                        to_nodes(S1, staged[:, :])

            def pick_rows(i, chunks):
                for c in chunks:
                    if c == 0:
                        if not first_iteration(i):
                            pe.wait_ge(S1["picked"], 2 * i - 1)
                        pe.wait_ge(S1["places_a"], i + 1)
                    if c == HALF:
                        pe.wait_ge(S1["places_b"], i + 1)
                    last = nc.tensor.matmul(ps_picked, lhsT=at_place[:, c, :], rhs=feats[:, c, :],
                                            start=(c == 0), stop=(c == CHUNKS - 1))
                    if c == HALF - 1:
                        last.then_inc(S1["half"], 1)
                    if c == CHUNKS - 1:
                        last.then_inc(S1["ten"], 1)

            def to_nodes(S, sums):
                for k in range(CB):
                    last = nc.tensor.matmul(ps_nodes[:, k * D:(k + 1) * D], lhsT=sums[:, k:k + (NP - 1) * CB + 1:CB],
                                            rhs=center_sb[:, :], start=True, stop=True)
                last.then_inc(S["nodes"], 1)

            def last_to_nodes(S, n):
                pe.wait_ge(S["acc"], GROUPS)
                to_nodes(S, acc[n][0:D, EARLY * CN:N])

            def windowed():
                layer(pe, steps0)
                output_layer(ITERS - 1, LAST + 1, 1)
                sum_messages(S0, ITERS - 1, LAST + 1, 1)
                last_to_nodes(S0, 0)
                pick_rows(0, range(CHUNKS))
                layer(pe, steps1)
                last_to_nodes(S1, 1)

            def merge_tiles(G, h, u):
                for t in range(TILES):
                    n = u * TILES + t
                    wait_count(pe, G["dst"], h, 2, u + 1)
                    wait_count(pe, G["same"], h, 2 * TILES, n)
                    nc.tensor.transpose(ps_row, dst_f[:, t:t + 1].to_broadcast([P, P]), ident_sb[:, :]).then_inc(G["row"], 1)
                    wait_count(pe, G["addend"], h, 2 * TILES, n)
                    wait_count(pe, G["msg"], h, 2, u + 1)
                    wait_count(pe, G["same"], h, 2 * TILES, n + 1)
                    nc.tensor.matmul(ps_merged, lhsT=same[:, :], rhs=msg[:, 0, t, :], start=True, stop=True).then_inc(G["merged"], 1)

            def general_steps0(h):
                for u in range(2):
                    pe.wait_ge(G0["edges"], h * 16 + 16)
                    wait_count(pe, G0["rows"], h, 64 * TILES, (u + 1) * 32 * TILES)
                    for t in range(TILES):
                        last = nc.tensor.transpose(ps_t[0][:, t * P:(t + 1) * P], edge[:, u, t, :], ident_sb[:, :])
                    last.then_inc(G0["trans"], 1)
                    wait_count(pe, G0["edgeT"], h, 2, u + 1)
                    nc.tensor.matmul(ps_h[0][:, :], lhsT=w_full[:, :], rhs=edgeT[:, 0, :], start=True, stop=True).then_inc(G0["pre"], 1)
                    wait_count(pe, G0["h"], h, 2, u + 1)
                    for t in range(TILES):
                        last = nc.tensor.matmul(ps_m[:, t, :], lhsT=hT[:, 0, t * P:(t + 1) * P], rhs=w2_sb[:, :], start=True, stop=True)
                    last.then_inc(G0["msgp"], 1)
                    merge_tiles(G0, h, u)

            def general_steps1(h):
                for u in range(2):
                    merge_tiles(G1, h, u)

            def general():
                pe.wait_ge(s_known, 2)
                peeled(pe, general_steps0, HALVES)
                peeled(pe, general_steps1, HALVES)

            by_width(pe, general, windowed)

        @block.vector
        def _(dve):
            def linked(s):
                count = [0]

                def link(ins):
                    count[0] += 1
                    ins.then_inc(s, 1)
                    dve.wait_ge(s, count[0])
                return link

            link = linked(s_prologue)
            nc.vector.memset(zeros[:, :], 0.0)
            nc.vector.memset(norm_eps[:, :], NORM_EPS)
            link(nc.vector.memset(ones[:, :], 1.0))
            dve.sem_inc(s_set, 1)
            dve.wait_ge(s_dst_g, 16)
            by_group = dst_g.rearrange("p (g e) -> p g e", g=UNROLL)
            link(nc.vector.tensor_reduce(low[:, :], by_group, AX.X, ALU.min))
            link(nc.vector.tensor_scalar(base[:, :], low[:, :], float(N - WIN), None, ALU.min))
            dve.wait_ge(s_ident, 16)
            nc.vector.tensor_tensor(spread[:, :, :], ident_sb[0:ITERS, 0:ITERS].unsqueeze(2).to_broadcast([ITERS, ITERS, UNROLL]),
                                    base[:, :].unsqueeze(1).to_broadcast([ITERS, ITERS, UNROLL]), ALU.mult).then_inc(s_spread, 1)
            dve.wait_ge(s_normed, 16)
            nc.vector.tensor_scalar(late[:, :], base[:, :], normed_sb[:, :], None, ALU.is_lt)
            link(nc.vector.tensor_reduce(high[:, :], by_group, AX.X, ALU.max))
            link(nc.vector.tensor_tensor(high[:, :], high[:, :], base[:, :], ALU.subtract))
            nc.vector.scalar_tensor_tensor(wide[:, :], high[:, :], float(WIN), late[:, :], ALU.is_ge, ALU.max).then_inc(s_wide, 1)
            dve.wait_ge(s_windows, 1)
            nc.vector.tensor_copy(base_row[:, :], ps_t[0][0:1, 0:SLOTS]).then_inc(s_known, 1)
            dve.wait_ge(s_n_wide, 1)
            link(nc.vector.tensor_reduce(n_wide[:, :], ps_t[1][0:1, 0:UNROLL], AX.X, ALU.add))
            nc.vector.tensor_copy(n_wide_i[:, :], n_wide[:, :]).then_inc(s_known, 1)
            dve.wait_ge(s_dst_t, 16)
            link(nc.vector.tensor_tensor(rel[:, :, :], dst_t.rearrange("p (g t) -> p g t", t=TILES),
                                         ps_t[0][:, 0:SLOTS].unsqueeze(2).to_broadcast([P, SLOTS, TILES]), ALU.subtract))
            dve.wait_ge(s_const, 16 * N_CONST)
            link(nc.vector.tensor_scalar(res_scale[:, :], res_scale[:, :], 2.0, None, ALU.add))

            def onehot(S, i, u, ahead=0):
                wait_group(dve, S["seg"], i, u, back=UNROLL - ahead)
                for t in range(TILES):
                    last = nc.vector.tensor_scalar(edge[:, (u + ahead) % UNROLL, t, 0:WIN], iota_sb[:, :],
                                                   rel[:, bass.ds(i * UNROLL + u + ahead, 1), t], None, ALU.is_equal)
                last.then_inc(S["onehot"], 1)

            def accumulate(S, n, i, u, back):
                first = dve.value_load(base_row[0:1, bass.ds(i * UNROLL + (u - back), 1)], min_val=0, max_val=N - WIN)
                wait_group(dve, S["acc"], i, u, back=back + 1)
                wait_group(dve, S["seg"], i, u, back=back)
                nc.vector.tensor_tensor(acc[n][0:D, bass.ds(first, WIN)], acc[n][0:D, bass.ds(first, WIN)], ps_s[:, :], ALU.add).then_inc(S["acc"], 1)

            def add_b2(done, slot):
                nc.vector.tensor_tensor(msg[:, slot, :, :], ps_m[:, :, :], b2_sb[:, :].unsqueeze(1).to_broadcast([P, TILES, D]),
                                        ALU.add).then_inc(done, 1)

            def offset_messages(i, u, back):
                wait_group(dve, S0["seg"], i, u, back=back + 2)
                wait_group(dve, S0["msgp"], i, u, back=back)
                add_b2(S0["msg"], (u - back) % 2)

            def steps0(i, c):
                nc.vector.tensor_copy(acc[1][0:D, bass.ds(i * P, P)], zeros[:, :])
                for u in groups_of(i):
                    wait_group(dve, S0["pre"], i, u, back=UNROLL)
                    wait_group(dve, S0["awin"], i, u)
                    nc.vector.tensor_copy(w_edge[0:WIN, u, :], ps_a[:, :]).then_inc(S0["stat"], 1)
                    if not last_group(i, u):
                        onehot(S0, i, u, ahead=1)
                    if not first_group(i, u):
                        offset_messages(i, u, 1)
                        accumulate(S0, 0, i, u, 1)
                    norm_steps(S0, c, u, in_psum, feats)

            def tenths(ins, place, done, count):
                nc.vector.tensor_scalar(place, ins, 1.0 / CB, 0.5 / CB - 0.5, ALU.mult, ALU.add).then_inc(done, 1)
                dve.wait_ge(done, count)
                nc.vector.tensor_scalar(place, place, ROUND, None, ALU.add).then_inc(done, 1)
                dve.wait_ge(done, count + 1)

            def find_rests():
                done = S1["rest"]
                tenths(src_col[:, :], col_place[:, :], done, 1)
                nc.vector.tensor_scalar(col_rest[:, :], col_place[:, :], -ROUND, -float(CB), ALU.add, ALU.mult).then_inc(done, 1)
                dve.wait_ge(done, 3)
                nc.vector.tensor_tensor(col_rest[:, :], col_rest[:, :], src_col[:, :], ALU.add).then_inc(done, 1)
                dve.wait_ge(done, 4)

            def one_hot_places(first, done):
                nc.vector.tensor_tensor(at_place[:, first:first + HALF, :], row_place[:, :].unsqueeze(1).to_broadcast([NP, HALF, P]),
                                        places_sb[:, first:first + HALF].unsqueeze(2).to_broadcast([NP, HALF, P]),
                                        ALU.is_equal).then_inc(done, 1)

            def places_a(i, row):
                if not first_iteration(i):
                    dve.wait_ge(S1["half"], i)
                tenths(row, row_place[:, :], S1["place"], 2 * i + 1)
                one_hot_places(0, S1["places_a"])

            def places_b(i):
                one_hot_places(HALF, S1["places_b"])

            def select_rows(i):
                dve.wait_ge(S1["ten"], i + 1)
                nc.vector.scalar_tensor_tensor(picked[:, :, :], iota_sb[:, 0:CB].unsqueeze(2).to_broadcast([P, CB, D]),
                                               col_rest[:, bass.ds(i, 1)], ps_picked.rearrange("p (k f) -> p k f", f=D),
                                               ALU.is_equal, ALU.mult).then_inc(S1["picked"], 1)
                dve.wait_ge(S1["picked"], 2 * i + 1)
                nc.vector.tensor_reduce(edge[:, PICK, TILES - 1, D:2 * D], picked[:, :, :].rearrange("p k f -> p f k"), AX.X,
                                        ALU.add).then_inc(S1["picked"], 1)

            def steps1(i, c):
                for u in groups_of(i):
                    if not last_group(i, u):
                        onehot(S1, i, u, ahead=1)
                    if c is not None and u == 2:
                        add_residual(S1, c)
                    if u == PICK:
                        dve.wait_ge(S1["src_row"], i * 16 + 16)
                        places_a(i + 2, src_row[:, :])
                    wait_group(dve, S1["msg"], i, u, back=2)
                    dve.wait_ge(S1["edges"][u // 2], i * 16 + 16)
                    dve.wait_ge(S1["rows"][u], i * (16 * gathered(S1, u)) + 16 * gathered(S1, u))
                    nc.vector.tensor_tensor(pre1[:, u % 2, :, :], edge[:, u, :, D:2 * D], e48_sb[:, u, :, :], ALU.add).then_inc(S1["sum"], 1)
                    if not first_group(i, u):
                        accumulate(S1, 1, i, u, 1)
                    if u == 0:
                        select_rows(i)
                        if not last_iteration(i):
                            places_b(i + 1)
                    norm_steps(S1, c, u, in_resid, resid)

            def as_nodes(t):
                return t.rearrange("p c (k f) -> p (c k) f", f=D)

            def flat(t):
                return t.rearrange("p c k -> p (c k)")

            def over_features(t):
                return flat(t).unsqueeze(2).to_broadcast([NP, CB, D])

            def add_residual(S, c):
                dve.wait_ge(S["nodes"], c + 1)
                nc.vector.scalar_tensor_tensor(one(resid, c), one(feats, c), res_scale[0:NP, :], ps_nodes.unsqueeze(1),
                                               ALU.mult, ALU.add).then_inc(S["resid"], 1)

            def sum_squares(S, c, slot):
                dve.wait_ge(S["square"], c + 1)
                nc.vector.tensor_reduce(flat(one(var, c)), as_nodes(square[:, slot:slot + 1, :]), AX.X, ALU.add).then_inc(S["var"], 1)

            def divide(S, c, centred, nodes):
                dve.wait_ge(S["std"], c + 1)
                nc.vector.reciprocal(one(rstd, c), one(std, c)).then_inc(S["rstd"], 1)
                dve.wait_ge(S["rstd"], c + 1)
                nc.vector.tensor_tensor(as_nodes(one(nodes, c)), centred, over_features(one(rstd, c)), ALU.mult).then_inc(S["norm"], 1)

            def in_psum(c):
                return ps_nodes.rearrange("p (k f) -> p k f", f=D)

            def in_resid(c):
                return as_nodes(one(resid, c))

            def norm_steps(S, c, u, centred, nodes):
                if c is not None and u == 2:
                    sum_squares(S, c, 0)
                if c is not None and u == 3:
                    divide(S, c, centred(c), nodes)

            def windowed():
                onehot(S0, 0, 0)
                dve.wait_ge(s_xT, 16)
                layer(dve, steps0)
                offset_messages(ITERS - 1, LAST + 1, 1)
                accumulate(S0, 0, ITERS - 1, LAST + 1, 1)
                onehot(S1, 0, 0)
                sum_squares(S0, EARLY, 0)
                divide(S0, EARLY, in_psum(EARLY), feats)
                places_a(0, first_rows[:, 0, :])
                places_b(0)
                find_rests()
                places_a(1, first_rows[:, 1, :])
                layer(dve, steps1)
                accumulate(S1, 1, ITERS - 1, LAST + 1, 1)
                dve.wait_ge(S1["places_a"], ITERS + 1)
                add_residual(S1, EARLY)
                sum_squares(S1, EARLY, 0)
                divide(S1, EARLY, in_resid(EARLY), resid)

            def general_layer(G, S, n, link):
                per_half = [0]

                def steps(h):
                    count = [0]

                    def step(ins):
                        count[0] += 1
                        ins.then_inc(G["step"], 1)
                        wait_count(dve, G["step"], h, per_half[0], count[0])

                    for u in range(2):
                        dst_of = dst_t[:, bass.ds(h * (2 * TILES) + u * TILES, TILES)]
                        if n == 0:
                            step(nc.vector.tensor_scalar(dst_idx[:, :], dst_of, 0.0, None, ALU.add))
                        nc.vector.tensor_scalar(dst_f[:, :], dst_of, 0.0, None, ALU.add).then_inc(G["dst"], 1)
                        if n == 0:
                            wait_count(dve, G["msgp"], h, 2, u + 1)
                            add_b2(G["msg"], 0)
                        else:
                            dve.wait_ge(G["edges"], h * 16 + 16)
                            wait_count(dve, G["rows"], h, 32 * TILES, (u + 1) * 16 * TILES)
                            nc.vector.tensor_tensor(pre1[:, 0, :, :], edge[:, u, :, D:2 * D], e48_sb[:, u, :, :], ALU.add).then_inc(G["sum"], 1)
                        for t in range(TILES):
                            m = u * TILES + t
                            wait_count(dve, G["dst"], h, 2, u + 1)
                            wait_count(dve, G["row"], h, 2 * TILES, m + 1)
                            nc.vector.tensor_scalar(same[:, :], ps_row, dst_f[:, t:t + 1], None, ALU.is_equal).then_inc(G["same"], 1)
                            wait_count(dve, G["same"], h, 2 * TILES, m + 1)
                            step(nc.vector.tensor_tensor(same_earlier[:, :], same[:, :], earlier_sb[:, :], ALU.mult))
                            step(nc.vector.tensor_reduce(n_earlier[:, :], same_earlier[:, :], AX.X, ALU.add))
                            step(nc.vector.tensor_tensor(to_spare[:, :], spare_sb[:, :], dst_f[:, t:t + 1], ALU.subtract))
                            step(nc.vector.scalar_tensor_tensor(to_spare[:, :], n_earlier[:, :], 0.0, to_spare[:, :], ALU.is_gt, ALU.mult))
                            wait_count(dve, G["added"], h, 32 * TILES, 16 * m)
                            step(nc.vector.tensor_tensor(target[:, :], to_spare[:, :], dst_f[:, t:t + 1], ALU.add))
                            wait_count(dve, G["merged"], h, 2 * TILES, m + 1)
                            nc.vector.tensor_copy(addend[:, :], ps_merged).then_inc(G["addend"], 1)
                    per_half[0] = count[0]

                def center(c):
                    r, f, m = one(resid, c), one(feats, c), one(mean, c)
                    if n == 0:
                        link(nc.vector.tensor_tensor(r, r, f, ALU.add))
                    else:
                        link(nc.vector.scalar_tensor_tensor(r, f, res_scale[0:NP, :], r, ALU.mult, ALU.add))
                    link(nc.vector.tensor_reduce(flat(m), as_nodes(r), AX.X, ALU.add))
                    link(nc.vector.tensor_scalar(m, m, 1.0 / D, None, ALU.mult))
                    nc.vector.tensor_tensor(as_nodes(r), as_nodes(r), over_features(m), ALU.subtract).then_inc(S["resid"], 1)

                nc.vector.memset(zero_table, 0.0).then_inc(G["zeroed"], 1)
                peeled(dve, steps, HALVES)
                dve.wait_ge(G["table"], 32)
                for c in range(CHUNKS + 1):
                    if c < CHUNKS:
                        center(c)
                        sum_squares(S, c, c % 2)
                    if c >= 1:
                        divide(S, c - 1, in_resid(c - 1), resid if n else feats)

            def general():
                link = linked(s_general)
                dve.wait_ge(s_x, 16)
                dve.wait_ge(s_xT, 16)
                general_layer(G0, S0, 0, link)
                dve.wait_ge(s_x1, 16 * CHUNKS)
                general_layer(G1, S1, 1, link)

            by_width(dve, general, windowed)


def kernel(**inputs):
    import numpy as np
    import concourse.bacc as bacc
    from concourse.bass_utils import run_bass_kernel_spmd

    x, src, dst = (np.asarray(inputs[k]) for k in ("x", "src", "dst"))
    e32, e48 = np.asarray(inputs["edge_attr_32"]), np.asarray(inputs["edge_attr_48"])

    def padded_rows(a, rows, fill):
        out = np.full((rows,) + a.shape[1:], fill, a.dtype)
        out[:a.shape[0]] = a
        return out

    def by_halves(a):
        f = a.shape[1]
        a = padded_rows(a, EPAD, 0).reshape(HALVES, 2, P, TILES * f)
        return np.ascontiguousarray(a.transpose(0, 2, 1, 3)).reshape(HALVES, P, 2 * TILES * f)

    def by_tiles(a, fill):
        a = padded_rows(a, EPAD, fill).reshape(SLOTS, P, TILES)
        return np.ascontiguousarray(a.transpose(1, 0, 2)).reshape(P, SLOTS * TILES)

    picked_src = np.ascontiguousarray(by_tiles(src, 0).reshape(P, ITERS, UNROLL, TILES)[:, :, PICK, TILES - 1])
    arrays = {
        "x": padded_rows(x, XROWS, 0),
        "xT": np.ascontiguousarray(x.T),
        "src_tiles": by_tiles(src, 0).view(np.uint32),
        "dst_tiles": by_tiles(dst, N),
        "dst_groups": padded_rows(dst, EPAD, dst[-1]).reshape(ITERS, UNROLL * GE),
        "e32": by_halves(e32),
        "e48": by_halves(e48),
        "w1": np.asarray(inputs["L0_gnn_W1"]),
        "w2": np.asarray(inputs["L0_gnn_W2"]),
        "b1": np.asarray(inputs["L0_gnn_b1"]).reshape(H, 1),
        "b2": np.asarray(inputs["L0_gnn_b2"]).reshape(1, D),
        "eps": np.asarray(inputs["L1_gnn_eps"]).reshape(1, 1),
        "ident": np.eye(P, dtype=np.float32),
        "iota": np.tile(np.arange(WIN, dtype=np.float32), (P, 1)),
        "center": (np.eye(D) - 1.0 / D).astype(np.float32),
        "normed": (np.clip(np.arange(ITERS) - NORM_ITER + 1, 0, EARLY) * np.float32(CN)).astype(np.float32).reshape(ITERS, 1),
        "src_rows": padded_rows(np.ascontiguousarray(picked_src.T), ITERS + 1, 0),
        "src_columns": picked_src,
        "places": (ROUND + NP * np.arange(CHUNKS) + np.arange(NP)[:, None]).astype(np.float32),
        "earlier": np.tril(np.ones((P, P), np.float32), -1),
        "spare": (N + 1 + np.arange(P, dtype=np.float32)).reshape(P, 1),
    }
    nc = bacc.Bacc("TRN2", target_bir_lowering=False, num_devices=1)
    args = [nc.dram_tensor(k, a.shape, mybir.dt.from_np(a.dtype), kind="ExternalInput").ap() for k, a in arrays.items()]
    out = nc.dram_tensor("out", (N, D), F32, kind="ExternalOutput").ap()
    build(nc, *args, out)
    return run_bass_kernel_spmd(nc, [arrays], core_ids=[0]).results[0]["out"]
```

```python
from contextlib import ExitStack

import concourse.bass as bass
from concourse import mybir

F32 = mybir.dt.float32
BF16 = mybir.dt.bfloat16
I32 = mybir.dt.int32
U32 = mybir.dt.uint32
ALU = mybir.AluOpType
ACT = mybir.ActivationFunctionType
AX = mybir.AxisListType

N = 12500
D = 48
DE = 32
H = 128
E = 200000
P = 128
TILES = 4
GE = P * TILES
UNROLL = 4
WIN = 48
GROUPS = -(-E // GE)
ITERS = -(-GROUPS // UNROLL)
LAST = GROUPS - 1 - (ITERS - 1) * UNROLL
SLOTS = ITERS * UNROLL
EPAD = SLOTS * GE
HALVES = SLOTS // 2
CHUNKS = 10
CN = N // CHUNKS
CB = 10
NP = CN // CB
PAIRS = SLOTS // 2
PARTS = 3
HB = CB // 2
PIECES = 2 * CHUNKS
EARLY = CHUNKS - 1
NORM_ITER = ITERS - 1 - 2 * EARLY
ACCW = P * ITERS
XROWS = N + 1
TROWS = -(-(XROWS + P) // P) * P
NORM_EPS = 1e-5
SHARES = (range(0, CHUNKS // 2), range(CHUNKS // 2, CHUNKS))
ROUND = 1.5 * 2 ** 23
assert CHUNKS * NP * CB == N and NP <= P and ACCW >= N and ITERS <= P and CB * D <= GE and WIN + D + DE == P
assert UNROLL * GE + SLOTS * TILES + TROWS // P * D <= ACCW


def build(nc, x, xT, src_tiles, dst_tiles, dst_groups, e32, e48, w1, w2, b1, b2, eps, ident, iota, center, normed,
          src_rows, src_columns, places, earlier, spare, out):
    ctx = ExitStack()
    with ctx:
        def sb(name, shape, dt=F32):
            return ctx.enter_context(nc.sbuf_tensor(name, shape, dt))

        def pb(name, shape, dt=F32):
            return ctx.enter_context(nc.psum_tensor(name, shape, dt))

        def sem(name):
            return ctx.enter_context(nc.semaphore(name))

        def sems(name, n):
            return [sem(f"{name}{k}") for k in range(n)]

        x1_dram = nc.dram_tensor("x1_dram", (N, D), F32, kind="Internal").ap()
        table = [nc.dram_tensor(f"table{n}_dram", (TROWS, D), F32, kind="Internal").ap() for n in range(2)]

        ident_sb = sb("ident_sb", [P, P])
        iota_sb = sb("iota_sb", [P, WIN])
        center_sb = sb("center_sb", [D, D])
        w1_dst = sb("w1_dst", [D, H])
        w2_sb = sb("w2_sb", [H, D])
        b1_sb = sb("b1_sb", [H, 1])
        b2_sb = sb("b2_sb", [P, D])
        res_scale = sb("res_scale", [P, 1])
        norm_eps = sb("norm_eps", [P, 1])
        root_eps = sb("root_eps", [P, 1])
        zeros = sb("zeros", [D, P])
        ones = sb("ones", [ITERS, P])
        low = sb("low", [ITERS, UNROLL])
        high = sb("high", [ITERS, UNROLL])
        base = sb("base", [ITERS, UNROLL])
        wide = sb("wide", [ITERS, UNROLL])
        normed_sb = sb("normed_sb", [ITERS, 1])
        late = sb("late", [ITERS, UNROLL])
        spread = sb("spread", [ITERS, ITERS, UNROLL])
        base_row = sb("base_row", [1, SLOTS], I32)
        n_wide = sb("n_wide", [1, 1])
        n_wide_i = sb("n_wide_i", [1, 1], I32)
        rel = sb("rel", [P, SLOTS, TILES])
        idx = sb("idx", [P, UNROLL, TILES], U32)
        edge = sb("edge", [P, UNROLL, TILES, P])
        e48_sb = sb("e48_sb", [P, UNROLL, TILES, D])
        x_win = sb("x_win", [D, UNROLL, WIN])
        w_edge = sb("w_edge", [P, UNROLL, H])
        edgeT = sb("edgeT", [P, 2, GE])
        hT = sb("hT", [H, 2, GE])
        pre1 = sb("pre1", [P, 2, TILES, D])
        msg = sb("msg", [P, 2, TILES, D])
        first_rows = sb("first_rows", [NP, 3, P], I32)
        src_row = sb("src_row", [NP, 2, P], I32)
        row_place = sb("row_place", [NP, P])
        places_sb = sb("places_sb", [NP, CHUNKS])
        at_place = sb("at_place", [NP, 2, CHUNKS, P], BF16)
        src_col = sb("src_col", [P, PAIRS], I32)
        col_place = sb("col_place", [P, PAIRS])
        col_rest = sb("col_rest", [P, PAIRS])
        picked = sb("picked", [P, CB, D])
        split_rest = sb("split_rest", [NP, 1, HB * D])
        acc = [sb("acc0", [P, ACCW]), sb("acc1", [P, ACCW])]
        x1_parts = (acc[0][0:NP, 0:N].rearrange("p (c n) -> p c n", c=CHUNKS)[:, :, 0:PARTS * CB * D // 2].bitcast(BF16)
                    .rearrange("p c (a n) -> p c a n", a=PARTS))
        dst_g = acc[1][0:ITERS, 0:UNROLL * GE].bitcast(I32)
        dst_t = acc[1][:, UNROLL * GE:UNROLL * GE + SLOTS * TILES].bitcast(I32)
        zero_table = acc[1][:, UNROLL * GE + SLOTS * TILES:UNROLL * GE + SLOTS * TILES + TROWS // P * D]
        staged = sb("staged", [D, CN])
        feats = sb("feats", [NP, PIECES, HB * D])
        resid = sb("resid", [NP, PIECES, HB * D])
        square = sb("square", [NP, 2, HB * D])
        mean = sb("mean", [NP, PIECES, HB])
        var = sb("var", [NP, PIECES, HB])
        std = sb("std", [NP, PIECES, HB])
        rstd = sb("rstd", [NP, PIECES, HB])
        dst_idx = sb("dst_idx", [P, TILES], U32)
        dst_f = sb("dst_f", [P, TILES])
        w_full = sb("w_full", [P, H])
        earlier_sb = sb("earlier_sb", [P, P])
        spare_sb = sb("spare_sb", [P, 1])
        same = sb("same", [P, P])
        same_earlier = sb("same_earlier", [P, P])
        n_earlier = sb("n_earlier", [P, 1])
        to_spare = sb("to_spare", [P, 1])
        target = sb("target", [P, 1], U32)
        addend = sb("addend", [P, D])

        ps_t = [pb(f"ps_t{k}", [P, GE]) for k in range(2)]
        ps_h = [pb(f"ps_h{k}", [H, GE]) for k in range(2)]
        ps_a = pb("ps_a", [WIN, H])
        ps_m = pb("ps_m", [P, TILES, D])
        ps_s = pb("ps_s", [D, WIN])
        ps_nodes = pb("ps_nodes", [P, GE])
        ps_picked = [ps[:, 0:CB * D] for ps in ps_h]
        ps_row, ps_merged = ps_t[1][:, 0:P], ps_h[1][:, 0:D]

        s_dst_g = sem("s_dst_g")
        s_dst_t = sem("s_dst_t")
        s_ident = sem("s_ident")
        s_normed = sem("s_normed")
        s_const = sem("s_const")
        s_set = sem("s_set")
        s_table = sem("s_table")
        s_spread = sem("s_spread")
        s_wide = sem("s_wide")
        s_windows = sem("s_windows")
        s_n_wide = sem("s_n_wide")
        s_known = sem("s_known")
        s_prologue = sem("s_prologue")
        s_general = sem("s_general")
        s_passed = sem("s_passed")
        s_xT = sem("s_xT")
        s_x = sem("s_x")
        s_x1 = sem("s_x1")
        s_out = sem("s_out")
        N_CONST = 19

        def layer_sems(n):
            per_slot = {"idx": 2, "edges": 2, "window": UNROLL, "rows": UNROLL, "src_row": 2}
            counts = ("onehot", "awin", "stat", "trans", "edgeT", "pre", "h", "msgp", "sum", "msg", "seg", "acc",
                      "parts", "place", "places", "rest", "ten", "picked", "staged", "nodes",
                      "resid", "square", "var", "std", "rstd", "norm")
            return {**{w: sems(f"s{n}_{w}", k) for w, k in per_slot.items()}, **{w: sem(f"s{n}_{w}") for w in counts}}

        def general_sems(n):
            counts = ("zeroed", "table", "idx", "edges", "dst", "rows", "trans", "edgeT", "pre", "h", "msgp", "sum",
                      "msg", "row", "same", "merged", "addend", "added", "step")
            return {w: sem(f"g{n}_{w}") for w in counts}

        S0, S1 = layer_sems(0), layer_sems(1)
        G0, G1 = general_sems(0), general_sems(1)
        block = ctx.enter_context(nc.Block())

        def wait_group(eng, s, i, u, back=0):
            if isinstance(i, int) and UNROLL * i + u - back < 0:
                return
            eng.wait_ge(s, i * UNROLL + (u - back + 1))

        def wait_count(eng, s, h, per, n):
            if isinstance(h, int) and per * h + n <= 0:
                return
            eng.wait_ge(s, h * per + n)

        def peeled(eng, body, count):
            body(0)
            with eng.Fori(1, count) as i:
                body(i)

        def layer(eng, body):
            body(0, None)
            with eng.Fori(1, NORM_ITER) as i:
                body(i, None)
            with eng.Fori(0, EARLY) as c:
                for h in range(2):
                    body(c * 2 + (NORM_ITER + h), (c, h))
            body(ITERS - 1, None)

        def number(piece, after=0):
            return piece[0] * 2 + (piece[1] + after)

        def gathered(S, u):
            return TILES - 1 if S is S1 and u % 2 else TILES

        def groups_of(i):
            return range(LAST + 1 if last_iteration(i) else UNROLL)

        def first_iteration(i):
            return isinstance(i, int) and i == 0

        def last_iteration(i):
            return isinstance(i, int) and i == ITERS - 1

        def first_group(i, u):
            return first_iteration(i) and u == 0

        def last_group(i, u):
            return last_iteration(i) and u == LAST

        def by_width(eng, general, windowed):
            eng.wait_ge(s_known, 2)
            wide_groups = eng.value_load(n_wide_i[0:1, 0:1], min_val=0, max_val=SLOTS)
            with eng.If(wide_groups > 0):
                general()
            with eng.Else():
                windowed()

        def one(t, piece):
            return t[:, bass.ds(number(piece), 1)]

        def nodes_in_psum(piece):
            bank = ps_t[0] if isinstance(piece[0], int) and piece[1] else ps_nodes
            return bank[0:NP, 0:HB * D].unsqueeze(1)

        def chunks_of(nodes):
            return nodes.rearrange("p (c h) n -> p c (h n)", h=2)

        def by_chunk(sums):
            return sums[0:D, 0:N].rearrange("d (c n) -> d c n", c=CHUNKS)

        def by_node(dram):
            return dram.rearrange("(c p k) f -> p c (k f)", c=CHUNKS, p=NP)

        def store_chunk(sp, n, c):
            S, dram, nodes, done = ((S0, x1_dram, feats, s_x1), (S1, out, resid, s_out))[n]
            sp.wait_ge(S["norm"], number((c, 1), 1))
            sp.dma_start(by_node(dram)[:, bass.ds(c, 1)], chunks_of(nodes)[:, bass.ds(c, 1)]).then_inc(done, 16)

        @block.sync
        def _(sp):
            def load_idx(done, i, h, slot):
                sp.dma_start(idx[:, slot:slot + 2, :].rearrange("p g t -> p (g t)"),
                             src_tiles[:, bass.ds(i * (UNROLL * TILES) + h * 2 * TILES, 2 * TILES)]).then_inc(done, 16)

            def next_idx(S, gathered_in, i, h):
                for u in (2 * h, 2 * h + 1):
                    sp.wait_ge(S["rows"][u], gathered_in * (16 * gathered(S, u)) + 16 * gathered(S, u))
                load_idx(S["idx"][h], i, h, 2 * h)

            def load_e32(done, half, slot):
                sp.dma_start(edge[:, slot:slot + 2, :, 2 * D:P].rearrange("p g t f -> p (g t) f"),
                             e32[bass.ds(half, 1), :, :].rearrange("a p (t f) -> (a p) t f", f=DE)).then_inc(done, 16)

            def load_e48(done, half, slot):
                sp.dma_start(e48_sb[:, slot:slot + 2, :, :].rearrange("p g t f -> p (g t f)"),
                             e48[bass.ds(half, 1), :, :].rearrange("a p n -> (a p) n")).then_inc(done, 16)

            load_idx(S0["idx"][0], 0, 0, 0)
            sp.dma_start(dst_g, dst_groups).then_inc(s_dst_g, 16)
            load_idx(S0["idx"][1], 0, 1, 2)
            sp.dma_start(dst_t, dst_tiles).then_inc(s_dst_t, 16)

            def loads0(i, c):
                for u in groups_of(i):
                    if u % 2 == 0:
                        wait_group(sp, S0["trans"], i, u + 1, back=UNROLL)
                        load_e32(S0["edges"][u // 2], i * 2 + u // 2, u)
                    if u == 0 and not first_iteration(i):
                        next_idx(S0, i - 1, i, 1)
                    wait_group(sp, S0["awin"], i, u, back=UNROLL)
                    first = sp.value_load(base_row[0:1, bass.ds(i * UNROLL + u, 1)], min_val=0, max_val=N - WIN)
                    sp.dma_start(x_win[:, u, :], xT[:, bass.ds(first, WIN)]).then_inc(S0["window"][u], 16)

                if not last_iteration(i):
                    next_idx(S0, i, i + 1, 0)
                if c is not None:
                    store_chunk(sp, 0, c)

            def loads1(i, c):
                for h in range(2):
                    wait_group(sp, S1["sum"], i, 2 * h + 1, back=UNROLL)
                    load_e48(S1["edges"][h], i * 2 + h, 2 * h)
                    if not last_iteration(i):
                        sp.dma_start(src_row[:, h, :], src_rows[bass.ds(i * 2 + (h + 3), 1), :].to_broadcast([NP, P])).then_inc(S1["src_row"][h], 16)
                    if h == 0 and not first_iteration(i):
                        next_idx(S1, i - 1, i, 1)
                if first_iteration(i):
                    store_chunk(sp, 0, EARLY)
                if not last_iteration(i):
                    next_idx(S1, i, i + 1, 0)
                if c is not None:
                    store_chunk(sp, 1, c)

            def loads_and_stores(loads):
                with sp.Fori(1, NORM_ITER + 2) as i:
                    loads(i, None)
                with sp.Fori(0, EARLY - 1) as c:
                    loads(c * 2 + (NORM_ITER + 2), c)
                    loads(c * 2 + (NORM_ITER + 3), None)
                loads(ITERS - 1, EARLY - 1)

            def windowed():
                loads0(0, None)
                loads_and_stores(loads0)
                sp.wait_ge(S0["trans"], GROUPS)
                load_idx(S1["idx"][0], 0, 0, 0)
                load_idx(S1["idx"][1], 0, 1, 2)
                loads1(0, None)
                loads_and_stores(loads1)
                store_chunk(sp, 1, EARLY)
                sp.wait_ge(s_x1, 16 * CHUNKS)
                sp.wait_ge(s_out, 16 * CHUNKS)

            def general_layer(G, n):
                def loads(h):
                    wait_count(sp, G["added"], h, 32 * TILES, 0)
                    sp.dma_start(idx[:, 0:2, :].rearrange("p g t -> p (g t)"),
                                 src_tiles[:, bass.ds(h * 2 * TILES, 2 * TILES)]).then_inc(G["idx"], 16)
                    (load_e48 if n else load_e32)(G["edges"], h, 0)

                sp.wait_ge(G["zeroed"], 1)
                sp.dma_start(table[n].rearrange("(p r) f -> p (r f)", p=P), zero_table).then_inc(G["table"], 16)
                peeled(sp, loads, HALVES)
                sp.wait_ge(G["added"], 16 * TILES * SLOTS)
                sp.wait_ge(G["table"], 16)
                sp.dma_start(chunks_of(resid), by_node(table[n][0:N, :])).then_inc(G["table"], 16)

            def general():
                for u in range(UNROLL):
                    sp.wait_ge(S0["rows"][u], 16 * TILES)
                sp.dma_start(chunks_of(feats), by_node(x[0:N, :])).then_inc(s_x, 16)
                general_layer(G0, 0)
                for c in range(CHUNKS):
                    store_chunk(sp, 0, c)
                sp.wait_ge(s_x1, 16 * CHUNKS)
                general_layer(G1, 1)
                for c in range(CHUNKS):
                    store_chunk(sp, 1, c)
                sp.wait_ge(s_out, 16 * CHUNKS)

            by_width(sp, general, windowed)

        @block.gpsimd
        def _(pool):
            def gather(cols, rows_of, index, done):
                pool.indirect_dma_start(out=cols, out_offset=None, in_=rows_of,
                                        in_offset=bass.IndirectOffsetOnAxis(ap=index, axis=0)).then_inc(done, 16)

            def gathers(S, rows_of, read, i):
                for u in groups_of(i):
                    pool.wait_ge(S["idx"][u // 2], i * 16 + 16)
                    wait_group(pool, S[read], i, u, back=UNROLL)
                    pool.sem_inc(s_passed, 1)
                    for t in range(gathered(S, u)):
                        gather(edge[:, u, t, D:2 * D], rows_of, idx[:, u, t:t + 1], S["rows"][u])

            gathers(S0, x, "trans", 0)

            def windowed():
                def others(S, rows_of, read):
                    with pool.Fori(1, ITERS - 1) as i:
                        gathers(S, rows_of, read, i)
                    gathers(S, rows_of, read, ITERS - 1)

                others(S0, x, "trans")
                pool.wait_ge(s_x1, 16 * CHUNKS)
                gathers(S1, x1_dram, "sum", 0)
                others(S1, x1_dram, "sum")

            def general_layer(G, n):
                def steps(h):
                    for u in range(2):
                        pool.wait_ge(G["idx"], h * 16 + 16)
                        wait_count(pool, G["dst"], h, 2, u + 1)
                        pool.sem_inc(s_passed, 1)
                        for t in range(TILES):
                            gather(edge[:, u, t, D:2 * D], x1_dram if n else x, idx[:, u, t:t + 1], G["rows"])
                            if n == 0:
                                gather(edge[:, u, t, 0:D], x, dst_idx[:, t:t + 1], G["rows"])
                        for t in range(TILES):
                            wait_count(pool, G["addend"], h, 2 * TILES, u * TILES + t + 1)
                            pool.sem_inc(s_passed, 1)
                            pool.indirect_dma_start(out=table[n], in_=addend[:, :], in_offset=None, compute_op=ALU.add,
                                                    out_offset=bass.IndirectOffsetOnAxis(ap=target[:, :], axis=0),
                                                    ).then_inc(G["added"], 16)

                pool.wait_ge(G["table"], 16)
                peeled(pool, steps, HALVES)

            def general():
                for u in range(UNROLL):
                    pool.wait_ge(S0["rows"][u], 16 * TILES)
                general_layer(G0, 0)
                pool.wait_ge(s_x1, 16 * CHUNKS)
                general_layer(G1, 1)

            by_width(pool, general, windowed)

        @block.scalar
        def _(act):
            act.dma_start(ident_sb[:, :], ident).then_inc(s_ident, 16)
            act.dma_start(normed_sb[:, :], normed).then_inc(s_normed, 16)
            for dst, src in ((iota_sb[:, :], iota), (w1_dst[:, :], w1[0:D, :]), (w2_sb[:, :], w2), (b1_sb[:, :], b1),
                             (places_sb[:, :], places), (src_col[:, :], src_columns),
                             (first_rows[:, 0, :], src_rows[0:1, :].to_broadcast([NP, P])),
                             (first_rows[:, 1, :], src_rows[1:2, :].to_broadcast([NP, P])),
                             (first_rows[:, 2, :], src_rows[2:3, :].to_broadcast([NP, P])),
                             (b2_sb[:, :], b2.to_broadcast([P, D])), (res_scale[:, :], eps.to_broadcast([P, 1])),
                             (center_sb[:, :], center), (w_full[:, :], w1), (earlier_sb[:, :], earlier),
                             (spare_sb[:, :], spare)):
                act.dma_start(dst, src).then_inc(s_const, 16)
            for u in range(UNROLL):
                act.dma_start(w_edge[D:P, u, :], w1[D:P, :]).then_inc(s_const, 16)
            act.dma_start(acc[0][0:D, 0:N], xT).then_inc(s_xT, 16)
            act.wait_ge(s_const, 16 * N_CONST)

            def squares(S, slot, centred):
                nc.scalar.activation(square[:, slot:slot + 1, :], centred, ACT.Square).then_inc(S["square"], 1)

            def deviations(S, c):
                act.wait_ge(S["var"], number(c, 1))
                nc.scalar.activation(one(std, c), one(var, c), ACT.Sqrt, bias=norm_eps[0:NP, :], scale=1.0 / D).then_inc(S["std"], 1)

            def squares_of_sums(n, S, c):
                act.wait_ge(S["resid" if n else "nodes"], number(c, 1))
                squares(S, c[1], one(resid, c) if n else nodes_in_psum(c))

            def norm_steps_after(n, S, i, c, u):
                if c is not None and c[1] == 0 and u == 0:
                    act.wait_ge(S["acc"], i * UNROLL)
                    nc.scalar.activation(staged[:, :].unsqueeze(1), by_chunk(acc[n])[:, bass.ds(c[0], 1), :],
                                         ACT.Copy).then_inc(S["staged"], 1)

            def steps0(i, c):
                for u in groups_of(i):
                    wait_group(act, S0["pre"], i, u, back=2)
                    wait_group(act, S0["trans"], i, u)
                    nc.scalar.activation(edgeT[:, u % 2, :], ps_t[u % 2][:, :], ACT.Copy).then_inc(S0["edgeT"], 1)
                    if c is not None and u == 2:
                        squares_of_sums(0, S0, c)
                    if c is not None and u == 3:
                        deviations(S0, c)
                    wait_group(act, S0["pre"], i, u, back=UNROLL)
                    wait_group(act, S0["awin"], i, u)
                    nc.scalar.activation(w_edge[0:WIN, u, :], ps_a[:, :], ACT.Copy).then_inc(S0["stat"], 1)
                    wait_group(act, S0["msgp"], i, u, back=2)
                    wait_group(act, S0["pre"], i, u)
                    nc.scalar.activation(hT[:, u % 2, :], ps_h[u % 2][:, :], ACT.Relu, bias=b1_sb[:, :]).then_inc(S0["h"], 1)
                    norm_steps_after(0, S0, i, c, u)

            def steps1(i, c):
                for u in groups_of(i):
                    if c is not None and u == 3:
                        squares_of_sums(1, S1, c)
                    wait_group(act, S1["seg"], i, u, back=2)
                    wait_group(act, S1["sum"], i, u)
                    nc.scalar.activation(msg[:, u % 2, :, :], pre1[:, u % 2, :, :], ACT.Relu).then_inc(S1["msg"], 1)
                    norm_steps_after(1, S1, i, c, u)
                    if c is not None and u == 3:
                        deviations(S1, c)

            def windowed():
                for n, S, steps in ((0, S0, steps0), (1, S1, steps1)):
                    layer(act, steps)
                    for h in range(2):
                        squares_of_sums(n, S, (EARLY, h))
                    for h in range(2):
                        deviations(S, (EARLY, h))

            def norm(S):
                for m in range(PIECES + 1):
                    if m < PIECES:
                        if m >= 2:
                            act.wait_ge(S["var"], m - 1)
                        act.wait_ge(S["resid"], m + 1)
                        squares(S, m % 2, one(resid, divmod(m, 2)))
                    if m >= 1:
                        deviations(S, divmod(m - 1, 2))

            def general_steps0(h):
                for u in range(2):
                    wait_count(act, G0["trans"], h, 2, u + 1)
                    nc.scalar.activation(edgeT[:, 0, :], ps_t[0][:, :], ACT.Copy).then_inc(G0["edgeT"], 1)
                    wait_count(act, G0["pre"], h, 2, u + 1)
                    nc.scalar.activation(hT[:, 0, :], ps_h[0][:, :], ACT.Relu, bias=b1_sb[:, :]).then_inc(G0["h"], 1)

            def general_steps1(h):
                for u in range(2):
                    wait_count(act, G1["sum"], h, 2, u + 1)
                    nc.scalar.activation(msg[:, 0, :, :], pre1[:, 0, :, :], ACT.Relu).then_inc(G1["msg"], 1)

            def general():
                peeled(act, general_steps0, HALVES)
                norm(S0)
                peeled(act, general_steps1, HALVES)
                norm(S1)

            act.wait_ge(s_set, 1)
            nc.scalar.activation(root_eps[:, :], norm_eps[:, :], ACT.Sqrt).then_inc(s_table, 1)
            act.wait_ge(s_table, 1)
            by_width(act, general, windowed)

        @block.tensor
        def _(pe):
            pe.wait_ge(s_set, 1)
            pe.wait_ge(s_spread, 1)
            nc.tensor.matmul(ps_t[0][:, 0:SLOTS], lhsT=ones[:, :], rhs=spread[:, :, :].rearrange("p q c -> p (q c)"),
                             start=True, stop=True).then_inc(s_windows, 1)
            pe.wait_ge(s_wide, 1)
            nc.tensor.matmul(ps_t[1][:, 0:UNROLL], lhsT=ones[:, :], rhs=wide[:, :], start=True, stop=True).then_inc(s_n_wide, 1)
            pe.wait_ge(s_ident, 16)
            pe.wait_ge(s_const, 16 * N_CONST)

            def sum_messages(S, i, u, back):
                wait_group(pe, S["acc"], i, u, back=back + 1)
                wait_group(pe, S["msg"], i, u, back=back)
                v = (u - back) % UNROLL
                for t in range(TILES):
                    last = nc.tensor.matmul(ps_s[:, :], lhsT=msg[:, v % 2, t, :], rhs=edge[:, v, t, 0:WIN],
                                            start=(t == 0), stop=(t == TILES - 1))
                last.then_inc(S["seg"], 1)

            def output_layer(i, u, back):
                v = (u - back) % UNROLL
                wait_group(pe, S0["msg"], i, u, back=back + 1)
                wait_group(pe, S0["h"], i, u, back=back)
                for t in range(TILES):
                    last = nc.tensor.matmul(ps_m[:, t, :], lhsT=hT[:, v % 2, t * P:(t + 1) * P], rhs=w2_sb[:, :],
                                            start=True, stop=True)
                last.then_inc(S0["msgp"], 1)

            def steps0(i, c):
                for u in groups_of(i):
                    pe.wait_ge(S0["window"][u], i * 16 + 16)
                    wait_group(pe, S0["stat"], i, u, back=1)
                    pe.wait_ge(S0["edges"][u // 2], i * 16 + 16)
                    wait_group(pe, S0["onehot"], i, u)
                    wait_group(pe, S0["edgeT"], i, u, back=2)
                    pe.wait_ge(S0["rows"][u], i * (16 * TILES) + 16 * TILES)
                    for t in range(TILES):
                        last = nc.tensor.transpose(ps_t[u % 2][:, t * P:(t + 1) * P], edge[:, u, t, :], ident_sb[:, :])
                    last.then_inc(S0["trans"], 1)
                    nc.tensor.matmul(ps_a[:, :], lhsT=x_win[:, u, :], rhs=w1_dst[:, :], start=True, stop=True).then_inc(S0["awin"], 1)
                    if not first_group(i, u):
                        output_layer(i, u, 1)
                    wait_group(pe, S0["stat"], i, u)
                    wait_group(pe, S0["h"], i, u, back=2)
                    wait_group(pe, S0["edgeT"], i, u)
                    nc.tensor.matmul(ps_h[u % 2][:, :], lhsT=w_edge[:, u, :], rhs=edgeT[:, u % 2, :], start=True, stop=True).then_inc(S0["pre"], 1)
                    if not first_group(i, u):
                        sum_messages(S0, i, u, 1)
                    if c is not None and u == 1:
                        pe.wait_ge(S0["staged"], c[0] + 1)
                        to_nodes(S0, staged[:, :], c)

            def steps1(i, c):
                for u in groups_of(i):
                    wait_group(pe, S1["onehot"], i, u)
                    sum_messages(S1, i, u, 0)
                    if c is not None and u == 1:
                        pe.wait_ge(S1["staged"], c[0] + 1)
                        to_nodes(S1, staged[:, :], c)
                    if not last_iteration(i):
                        pick_rows(i * 2 + (u // 2 + 2), u // 2, SHARES[u % 2])

            def pick_rows(q, odd, chunks):
                if 0 in chunks:
                    pe.wait_ge(S1["places"], q + 1)
                for c in chunks:
                    for part in range(PARTS):
                        last = nc.tensor.matmul(ps_picked[odd], lhsT=at_place[:, odd, c, :], rhs=x1_parts[:, c, part, :],
                                                start=(c == 0 and part == 0), stop=(c == CHUNKS - 1 and part == PARTS - 1))
                if CHUNKS - 1 in chunks:
                    last.then_inc(S1["ten"], 1)

            def to_nodes(S, sums, c):
                for k in range(HB):
                    first = c[1] * HB + k
                    last = nc.tensor.matmul(nodes_in_psum(c)[:, 0, k * D:(k + 1) * D], lhsT=sums[:, first:first + (NP - 1) * CB + 1:CB],
                                            rhs=center_sb[:, :], start=True, stop=True)
                last.then_inc(S["nodes"], 1)

            def last_to_nodes(S, n):
                pe.wait_ge(S["acc"], GROUPS)
                for h in range(2):
                    to_nodes(S, acc[n][0:D, EARLY * CN:N], (EARLY, h))

            def windowed():
                layer(pe, steps0)
                output_layer(ITERS - 1, LAST + 1, 1)
                sum_messages(S0, ITERS - 1, LAST + 1, 1)
                last_to_nodes(S0, 0)
                pe.wait_ge(S0["parts"], 4 * PIECES)
                pick_rows(0, 0, range(CHUNKS))
                pick_rows(1, 1, range(CHUNKS))
                layer(pe, steps1)
                last_to_nodes(S1, 1)

            def merge_tiles(G, h, u):
                for t in range(TILES):
                    n = u * TILES + t
                    wait_count(pe, G["dst"], h, 2, u + 1)
                    wait_count(pe, G["same"], h, 2 * TILES, n)
                    nc.tensor.transpose(ps_row, dst_f[:, t:t + 1].to_broadcast([P, P]), ident_sb[:, :]).then_inc(G["row"], 1)
                    wait_count(pe, G["addend"], h, 2 * TILES, n)
                    wait_count(pe, G["msg"], h, 2, u + 1)
                    wait_count(pe, G["same"], h, 2 * TILES, n + 1)
                    nc.tensor.matmul(ps_merged, lhsT=same[:, :], rhs=msg[:, 0, t, :], start=True, stop=True).then_inc(G["merged"], 1)

            def general_steps0(h):
                for u in range(2):
                    pe.wait_ge(G0["edges"], h * 16 + 16)
                    wait_count(pe, G0["rows"], h, 64 * TILES, (u + 1) * 32 * TILES)
                    for t in range(TILES):
                        last = nc.tensor.transpose(ps_t[0][:, t * P:(t + 1) * P], edge[:, u, t, :], ident_sb[:, :])
                    last.then_inc(G0["trans"], 1)
                    wait_count(pe, G0["edgeT"], h, 2, u + 1)
                    nc.tensor.matmul(ps_h[0][:, :], lhsT=w_full[:, :], rhs=edgeT[:, 0, :], start=True, stop=True).then_inc(G0["pre"], 1)
                    wait_count(pe, G0["h"], h, 2, u + 1)
                    for t in range(TILES):
                        last = nc.tensor.matmul(ps_m[:, t, :], lhsT=hT[:, 0, t * P:(t + 1) * P], rhs=w2_sb[:, :], start=True, stop=True)
                    last.then_inc(G0["msgp"], 1)
                    merge_tiles(G0, h, u)

            def general_steps1(h):
                for u in range(2):
                    merge_tiles(G1, h, u)

            def general():
                pe.wait_ge(s_known, 2)
                peeled(pe, general_steps0, HALVES)
                peeled(pe, general_steps1, HALVES)

            by_width(pe, general, windowed)

        @block.vector
        def _(dve):
            def linked(s):
                count = [0]

                def link(ins):
                    count[0] += 1
                    ins.then_inc(s, 1)
                    dve.wait_ge(s, count[0])
                return link

            link = linked(s_prologue)
            nc.vector.memset(zeros[:, :], 0.0)
            nc.vector.memset(norm_eps[:, :], NORM_EPS)
            link(nc.vector.memset(ones[:, :], 1.0))
            dve.sem_inc(s_set, 1)
            dve.wait_ge(s_dst_g, 16)
            by_group = dst_g.rearrange("p (g e) -> p g e", g=UNROLL)
            link(nc.vector.tensor_reduce(low[:, :], by_group, AX.X, ALU.min))
            link(nc.vector.tensor_scalar(base[:, :], low[:, :], float(N - WIN), None, ALU.min))
            dve.wait_ge(s_ident, 16)
            nc.vector.tensor_tensor(spread[:, :, :], ident_sb[0:ITERS, 0:ITERS].unsqueeze(2).to_broadcast([ITERS, ITERS, UNROLL]),
                                    base[:, :].unsqueeze(1).to_broadcast([ITERS, ITERS, UNROLL]), ALU.mult).then_inc(s_spread, 1)
            dve.wait_ge(s_normed, 16)
            nc.vector.tensor_scalar(late[:, :], base[:, :], normed_sb[:, :], None, ALU.is_lt)
            link(nc.vector.tensor_reduce(high[:, :], by_group, AX.X, ALU.max))
            link(nc.vector.tensor_tensor(high[:, :], high[:, :], base[:, :], ALU.subtract))
            nc.vector.scalar_tensor_tensor(wide[:, :], high[:, :], float(WIN), late[:, :], ALU.is_ge, ALU.max).then_inc(s_wide, 1)
            dve.wait_ge(s_windows, 1)
            nc.vector.tensor_copy(base_row[:, :], ps_t[0][0:1, 0:SLOTS]).then_inc(s_known, 1)
            dve.wait_ge(s_n_wide, 1)
            link(nc.vector.tensor_reduce(n_wide[:, :], ps_t[1][0:1, 0:UNROLL], AX.X, ALU.add))
            nc.vector.tensor_copy(n_wide_i[:, :], n_wide[:, :]).then_inc(s_known, 1)
            dve.wait_ge(s_dst_t, 16)
            link(nc.vector.tensor_tensor(rel[:, :, :], dst_t.rearrange("p (g t) -> p g t", t=TILES),
                                         ps_t[0][:, 0:SLOTS].unsqueeze(2).to_broadcast([P, SLOTS, TILES]), ALU.subtract))
            dve.wait_ge(s_const, 16 * N_CONST)
            link(nc.vector.tensor_scalar(res_scale[:, :], res_scale[:, :], 2.0, None, ALU.add))

            def onehot(S, i, u, ahead=0):
                wait_group(dve, S["seg"], i, u, back=UNROLL - ahead)
                for t in range(TILES):
                    last = nc.vector.tensor_scalar(edge[:, (u + ahead) % UNROLL, t, 0:WIN], iota_sb[:, :],
                                                   rel[:, bass.ds(i * UNROLL + u + ahead, 1), t], None, ALU.is_equal)
                last.then_inc(S["onehot"], 1)

            def accumulate(S, n, i, u, back):
                first = dve.value_load(base_row[0:1, bass.ds(i * UNROLL + (u - back), 1)], min_val=0, max_val=N - WIN)
                wait_group(dve, S["acc"], i, u, back=back + 1)
                wait_group(dve, S["seg"], i, u, back=back)
                nc.vector.tensor_tensor(acc[n][0:D, bass.ds(first, WIN)], acc[n][0:D, bass.ds(first, WIN)], ps_s[:, :], ALU.add).then_inc(S["acc"], 1)

            def add_b2(done, slot):
                nc.vector.tensor_tensor(msg[:, slot, :, :], ps_m[:, :, :], b2_sb[:, :].unsqueeze(1).to_broadcast([P, TILES, D]),
                                        ALU.add).then_inc(done, 1)

            def offset_messages(i, u, back):
                wait_group(dve, S0["seg"], i, u, back=back + 2)
                wait_group(dve, S0["msgp"], i, u, back=back)
                add_b2(S0["msg"], (u - back) % 2)

            def steps0(i, c):
                nc.vector.tensor_copy(acc[1][0:D, bass.ds(i * P, P)], zeros[:, :])
                for u in groups_of(i):
                    if not last_group(i, u):
                        onehot(S0, i, u, ahead=1)
                    if not first_group(i, u):
                        offset_messages(i, u, 1)
                    norm_steps(S0, c, u, in_psum, feats)
                    if not first_group(i, u):
                        accumulate(S0, 0, i, u, 1)

            def tenths(ins, place, done, count):
                nc.vector.tensor_scalar(place, ins, 1.0 / CB, 0.5 / CB - 0.5, ALU.mult, ALU.add).then_inc(done, 1)
                dve.wait_ge(done, count)
                nc.vector.tensor_scalar(place, place, ROUND, None, ALU.add).then_inc(done, 1)
                dve.wait_ge(done, count + 1)

            def find_rests():
                done = S1["rest"]
                tenths(src_col[:, :], col_place[:, :], done, 1)
                nc.vector.tensor_scalar(col_rest[:, :], col_place[:, :], -ROUND, -float(CB), ALU.add, ALU.mult).then_inc(done, 1)
                dve.wait_ge(done, 3)
                nc.vector.tensor_tensor(col_rest[:, :], col_rest[:, :], src_col[:, :], ALU.add).then_inc(done, 1)
                dve.wait_ge(done, 4)

            def find_places(q, odd, row):
                if not isinstance(q, int) or q >= 2:
                    dve.wait_ge(S1["ten"], q - 1)
                tenths(row, row_place[:, :], S1["place"], q * 2 + 1)
                nc.vector.tensor_tensor(at_place[:, odd, :, :], row_place[:, :].unsqueeze(1).to_broadcast([NP, CHUNKS, P]),
                                        places_sb[:, :].unsqueeze(2).to_broadcast([NP, CHUNKS, P]), ALU.is_equal).then_inc(S1["places"], 1)

            def select_rows(q, odd, u):
                dve.wait_ge(S1["ten"], q + 1)
                nc.vector.scalar_tensor_tensor(picked[:, :, :], iota_sb[:, 0:CB].unsqueeze(2).to_broadcast([P, CB, D]),
                                               col_rest[:, bass.ds(q, 1)], ps_picked[odd].rearrange("p (k f) -> p k f", f=D),
                                               ALU.is_equal, ALU.mult).then_inc(S1["picked"], 1)
                dve.wait_ge(S1["picked"], q * 2 + 1)
                nc.vector.tensor_reduce(edge[:, u, TILES - 1, D:2 * D], picked[:, :, :].rearrange("p k f -> p f k"), AX.X,
                                        ALU.add).then_inc(S1["picked"], 1)

            def steps1(i, c):
                for u in groups_of(i):
                    if not last_group(i, u):
                        onehot(S1, i, u, ahead=1)
                    if u % 2 == 0 and u + 1 in groups_of(i):
                        select_rows(i * 2 + u // 2, u // 2, u + 1)
                    if u % 2 and not last_iteration(i):
                        dve.wait_ge(S1["src_row"][u // 2], i * 16 + 16)
                        find_places(i * 2 + (u // 2 + 3), (u // 2 + 1) % 2, src_row[:, u // 2, :])
                    if u % 2:
                        dve.wait_ge(S1["picked"], i * 4 + (2 * (u // 2) + 2))
                    wait_group(dve, S1["msg"], i, u, back=2)
                    dve.wait_ge(S1["edges"][u // 2], i * 16 + 16)
                    dve.wait_ge(S1["rows"][u], i * (16 * gathered(S1, u)) + 16 * gathered(S1, u))
                    nc.vector.tensor_tensor(pre1[:, u % 2, :, :], edge[:, u, :, D:2 * D], e48_sb[:, u, :, :], ALU.add).then_inc(S1["sum"], 1)
                    if not first_group(i, u):
                        accumulate(S1, 1, i, u, 1)
                    norm_steps(S1, c, u, in_resid, resid)

            def as_nodes(t):
                return t.rearrange("p c (k f) -> p (c k) f", f=D)

            def flat(t):
                return t.rearrange("p c k -> p (c k)")

            def over_features(t):
                return flat(t).unsqueeze(2).to_broadcast([NP, HB, D])

            def add_residual(S, c):
                dve.wait_ge(S["nodes"], number(c, 1))
                nc.vector.scalar_tensor_tensor(one(resid, c), one(feats, c), res_scale[0:NP, :], nodes_in_psum(c),
                                               ALU.mult, ALU.add).then_inc(S["resid"], 1)

            def sum_squares(S, c):
                dve.wait_ge(S["square"], number(c, 1))
                nc.vector.tensor_reduce(flat(one(var, c)), as_nodes(square[:, c[1]:c[1] + 1, :]), AX.X, ALU.add).then_inc(S["var"], 1)

            def divide(S, c, centred, nodes):
                dve.wait_ge(S["std"], number(c, 1))
                nc.vector.reciprocal(one(rstd, c), one(std, c)).then_inc(S["rstd"], 1)
                dve.wait_ge(S["rstd"], number(c, 1))
                nc.vector.tensor_tensor(as_nodes(one(nodes, c)), centred, over_features(one(rstd, c)), ALU.mult).then_inc(S["norm"], 1)

            def in_psum(c):
                return as_nodes(nodes_in_psum(c))

            def in_resid(c):
                return as_nodes(one(resid, c))

            def split(c):
                x1, rest, done = one(feats, c), split_rest[:, :, :], S0["parts"]
                part = [x1_parts[:, bass.ds(c[0], 1), a, c[1] * HB * D:(c[1] + 1) * HB * D] for a in range(PARTS)]
                dve.wait_ge(S0["norm"], number(c, 1))
                nc.vector.tensor_scalar(part[0], x1, 0.0, None, ALU.add).then_inc(done, 1)
                dve.wait_ge(done, number(c) * 4 + 1)
                nc.vector.tensor_tensor(rest, x1, part[0], ALU.subtract).then_inc(done, 1)
                dve.wait_ge(done, number(c) * 4 + 2)
                nc.vector.tensor_scalar(part[1], rest, 0.0, None, ALU.add).then_inc(done, 1)
                dve.wait_ge(done, number(c) * 4 + 3)
                nc.vector.tensor_tensor(part[2], rest, part[1], ALU.subtract).then_inc(done, 1)

            def norm_steps(S, c, u, centred, nodes):
                if c is not None and u == 2 and S is S1:
                    add_residual(S, c)
                if c is not None and u == (2 if S is S0 else 3):
                    sum_squares(S, c)
                if c is not None and u == 3:
                    divide(S, c, centred(c), nodes)
                    if nodes is feats:
                        split(c)

            def windowed():
                onehot(S0, 0, 0)
                dve.wait_ge(s_xT, 16)
                layer(dve, steps0)
                offset_messages(ITERS - 1, LAST + 1, 1)
                accumulate(S0, 0, ITERS - 1, LAST + 1, 1)
                onehot(S1, 0, 0)
                for h in range(2):
                    sum_squares(S0, (EARLY, h))
                for h in range(2):
                    divide(S0, (EARLY, h), in_psum((EARLY, h)), feats)
                find_places(0, 0, first_rows[:, 0, :])
                for h in range(2):
                    split((EARLY, h))
                find_places(1, 1, first_rows[:, 1, :])
                find_rests()
                find_places(2, 0, first_rows[:, 2, :])
                layer(dve, steps1)
                accumulate(S1, 1, ITERS - 1, LAST + 1, 1)
                dve.wait_ge(S1["ten"], PAIRS)
                dve.wait_ge(S1["places"], PAIRS + 1)
                for h in range(2):
                    add_residual(S1, (EARLY, h))
                for h in range(2):
                    sum_squares(S1, (EARLY, h))
                for h in range(2):
                    divide(S1, (EARLY, h), in_resid((EARLY, h)), resid)

            def general_layer(G, S, n, link):
                per_half = [0]

                def steps(h):
                    count = [0]

                    def step(ins):
                        count[0] += 1
                        ins.then_inc(G["step"], 1)
                        wait_count(dve, G["step"], h, per_half[0], count[0])

                    for u in range(2):
                        dst_of = dst_t[:, bass.ds(h * (2 * TILES) + u * TILES, TILES)]
                        if n == 0:
                            step(nc.vector.tensor_scalar(dst_idx[:, :], dst_of, 0.0, None, ALU.add))
                        nc.vector.tensor_scalar(dst_f[:, :], dst_of, 0.0, None, ALU.add).then_inc(G["dst"], 1)
                        if n == 0:
                            wait_count(dve, G["msgp"], h, 2, u + 1)
                            add_b2(G["msg"], 0)
                        else:
                            dve.wait_ge(G["edges"], h * 16 + 16)
                            wait_count(dve, G["rows"], h, 32 * TILES, (u + 1) * 16 * TILES)
                            nc.vector.tensor_tensor(pre1[:, 0, :, :], edge[:, u, :, D:2 * D], e48_sb[:, u, :, :], ALU.add).then_inc(G["sum"], 1)
                        for t in range(TILES):
                            m = u * TILES + t
                            wait_count(dve, G["dst"], h, 2, u + 1)
                            wait_count(dve, G["row"], h, 2 * TILES, m + 1)
                            nc.vector.tensor_scalar(same[:, :], ps_row, dst_f[:, t:t + 1], None, ALU.is_equal).then_inc(G["same"], 1)
                            wait_count(dve, G["same"], h, 2 * TILES, m + 1)
                            step(nc.vector.tensor_tensor(same_earlier[:, :], same[:, :], earlier_sb[:, :], ALU.mult))
                            step(nc.vector.tensor_reduce(n_earlier[:, :], same_earlier[:, :], AX.X, ALU.add))
                            step(nc.vector.tensor_tensor(to_spare[:, :], spare_sb[:, :], dst_f[:, t:t + 1], ALU.subtract))
                            step(nc.vector.scalar_tensor_tensor(to_spare[:, :], n_earlier[:, :], 0.0, to_spare[:, :], ALU.is_gt, ALU.mult))
                            wait_count(dve, G["added"], h, 32 * TILES, 16 * m)
                            step(nc.vector.tensor_tensor(target[:, :], to_spare[:, :], dst_f[:, t:t + 1], ALU.add))
                            wait_count(dve, G["merged"], h, 2 * TILES, m + 1)
                            nc.vector.tensor_copy(addend[:, :], ps_merged).then_inc(G["addend"], 1)
                    per_half[0] = count[0]

                def center(c):
                    r, f, m = one(resid, c), one(feats, c), one(mean, c)
                    if n == 0:
                        link(nc.vector.tensor_tensor(r, r, f, ALU.add))
                    else:
                        link(nc.vector.scalar_tensor_tensor(r, f, res_scale[0:NP, :], r, ALU.mult, ALU.add))
                    link(nc.vector.tensor_reduce(flat(m), as_nodes(r), AX.X, ALU.add))
                    link(nc.vector.tensor_scalar(m, m, 1.0 / D, None, ALU.mult))
                    nc.vector.tensor_tensor(as_nodes(r), as_nodes(r), over_features(m), ALU.subtract).then_inc(S["resid"], 1)

                nc.vector.memset(zero_table, 0.0).then_inc(G["zeroed"], 1)
                peeled(dve, steps, HALVES)
                dve.wait_ge(G["table"], 32)
                for m in range(PIECES + 1):
                    if m < PIECES:
                        center(divmod(m, 2))
                        sum_squares(S, divmod(m, 2))
                    if m >= 1:
                        last = divmod(m - 1, 2)
                        divide(S, last, in_resid(last), resid if n else feats)

            def general():
                link = linked(s_general)
                dve.wait_ge(s_x, 16)
                dve.wait_ge(s_xT, 16)
                general_layer(G0, S0, 0, link)
                dve.wait_ge(s_x1, 16 * CHUNKS)
                general_layer(G1, S1, 1, link)

            by_width(dve, general, windowed)


def kernel(**inputs):
    import numpy as np
    import concourse.bacc as bacc
    from concourse.bass_utils import run_bass_kernel_spmd

    x, src, dst = (np.asarray(inputs[k]) for k in ("x", "src", "dst"))
    e32, e48 = np.asarray(inputs["edge_attr_32"]), np.asarray(inputs["edge_attr_48"])

    def padded_rows(a, rows, fill):
        out = np.full((rows,) + a.shape[1:], fill, a.dtype)
        out[:a.shape[0]] = a
        return out

    def by_halves(a):
        f = a.shape[1]
        a = padded_rows(a, EPAD, 0).reshape(HALVES, 2, P, TILES * f)
        return np.ascontiguousarray(a.transpose(0, 2, 1, 3)).reshape(HALVES, P, 2 * TILES * f)

    def by_tiles(a, fill):
        a = padded_rows(a, EPAD, fill).reshape(SLOTS, P, TILES)
        return np.ascontiguousarray(a.transpose(1, 0, 2)).reshape(P, SLOTS * TILES)

    picked_src = np.ascontiguousarray(by_tiles(src, 0).reshape(P, PAIRS, 2, TILES)[:, :, 1, TILES - 1])
    arrays = {
        "x": padded_rows(x, XROWS, 0),
        "xT": np.ascontiguousarray(x.T),
        "src_tiles": by_tiles(src, 0).view(np.uint32),
        "dst_tiles": by_tiles(dst, N),
        "dst_groups": padded_rows(dst, EPAD, dst[-1]).reshape(ITERS, UNROLL * GE),
        "e32": by_halves(e32),
        "e48": by_halves(e48),
        "w1": np.asarray(inputs["L0_gnn_W1"]),
        "w2": np.asarray(inputs["L0_gnn_W2"]),
        "b1": np.asarray(inputs["L0_gnn_b1"]).reshape(H, 1),
        "b2": np.asarray(inputs["L0_gnn_b2"]).reshape(1, D),
        "eps": np.asarray(inputs["L1_gnn_eps"]).reshape(1, 1),
        "ident": np.eye(P, dtype=np.float32),
        "iota": np.tile(np.arange(WIN, dtype=np.float32), (P, 1)),
        "center": (np.eye(D) - 1.0 / D).astype(np.float32),
        "normed": (np.clip((np.arange(ITERS) - NORM_ITER) // 2 + 1, 0, EARLY) * np.float32(CN)).astype(np.float32).reshape(ITERS, 1),
        "src_rows": padded_rows(np.ascontiguousarray(picked_src.T), PAIRS + 1, 0),
        "src_columns": picked_src,
        "places": (ROUND + NP * np.arange(CHUNKS) + np.arange(NP)[:, None]).astype(np.float32),
        "earlier": np.tril(np.ones((P, P), np.float32), -1),
        "spare": (N + 1 + np.arange(P, dtype=np.float32)).reshape(P, 1),
    }
    nc = bacc.Bacc("TRN2", target_bir_lowering=False, num_devices=1)
    args = [nc.dram_tensor(k, a.shape, mybir.dt.from_np(a.dtype), kind="ExternalInput").ap() for k, a in arrays.items()]
    out = nc.dram_tensor("out", (N, D), F32, kind="ExternalOutput").ap()
    build(nc, *args, out)
    return run_bass_kernel_spmd(nc, [arrays], core_ids=[0]).results[0]["out"]
```
